# Optimizing a Trainium2 kernel written in Bass

```python
import numpy as np
import jax
import jax.numpy as jnp

def _softmax(x, axis=-1):
    return jax.nn.softmax(x, axis=axis)

def _gelu(x):
    return jax.nn.gelu(x, approximate=True)

def _silu(x):
    return jax.nn.silu(x)

def _sigmoid(x):
    return jax.nn.sigmoid(x)

def _layernorm(x, axis=-1, eps=1e-05):
    m = jnp.mean(x, axis=axis, keepdims=True)
    v = jnp.var(x, axis=axis, keepdims=True)
    return (x - m) / jnp.sqrt(v + eps)

def _scatter_add(tgt, idx, src, axis=0):
    return tgt.at[idx].add(src)

def _segment_sum(src, seg, n):
    return jax.ops.segment_sum(src, seg, n)
kernel_name = 'mk_cond_seq_d2_seqx_r4_2fb039'

def setup_inputs(seed: int=0):
    np.random.seed(seed)
    _w = jnp.asarray

    def _rec_inputs():
        import jax
        import jax.numpy as jnp
        _rk = jax.random.key(seed)
        x = 7.22e-05 + 1 * jax.random.normal(jax.random.fold_in(_rk, 1), (32, 256, 256), jnp.float32)
        _lenS = 256 - jax.random.randint(jax.random.fold_in(_rk, 7), (32,), 0, max(1, 256 // 4) + 1, jnp.int32)
        _lenS2 = 256 - jax.random.randint(jax.random.fold_in(_rk, 8), (32,), 0, max(1, 256 // 4) + 1, jnp.int32)
        cond_1024 = 0.0061147 + 1.02565 * jax.random.normal(jax.random.fold_in(_rk, 11), (32, 256), jnp.float32)
        return (x, cond_1024)
    x, cond_1024 = _rec_inputs()

    def _L0_cond_setup():
        import jax, jax.numpy as jnp
        import numpy as np
        DIM = 256
        MLP_RATIO = 4
        EPS = 1e-06

        def rmsnorm(x, w):
            return x * jax.lax.rsqrt(jnp.mean(x * x, axis=-1, keepdims=True) + EPS) * w

        def film(x, cond, w, b):
            ss = cond @ w + b
            scale, shift = jnp.split(ss, 2, axis=-1)
            return x * (1.0 + scale[:, None, :]) + shift[:, None, :]
        key = jax.random.key(seed)
        ks = jax.random.split(key, 16)
        B, N, D = (4, 512, DIM)
        H = D * MLP_RATIO
        s = lambda fan_in: 1.0 / np.sqrt(fan_in)
        return {'x': jax.random.normal(ks[0], (B, N, D), jnp.float32), 'cond': jax.random.normal(ks[1], (B, D), jnp.float32), 'norm1_w': jnp.ones((D,), jnp.float32), 'film1_w': jax.random.normal(ks[2], (D, 2 * D), jnp.float32) * s(D), 'film1_b': jnp.zeros((2 * D,), jnp.float32), 'q_w': jax.random.normal(ks[3], (D, D), jnp.float32) * s(D), 'q_b': jnp.zeros((D,), jnp.float32), 'k_w': jax.random.normal(ks[4], (D, D), jnp.float32) * s(D), 'k_b': jnp.zeros((D,), jnp.float32), 'v_w': jax.random.normal(ks[5], (D, D), jnp.float32) * s(D), 'v_b': jnp.zeros((D,), jnp.float32), 'proj_w': jax.random.normal(ks[6], (D, D), jnp.float32) * s(D), 'proj_b': jnp.zeros((D,), jnp.float32), 'norm2_w': jnp.ones((D,), jnp.float32), 'film2_w': jax.random.normal(ks[7], (D, 2 * D), jnp.float32) * s(D), 'film2_b': jnp.zeros((2 * D,), jnp.float32), 'mlp_w1': jax.random.normal(ks[8], (D, H), jnp.float32) * s(D), 'mlp_b1': jnp.zeros((H,), jnp.float32), 'mlp_w2': jax.random.normal(ks[9], (H, D), jnp.float32) * s(H), 'mlp_b2': jnp.zeros((D,), jnp.float32)}
    _L0_cond_all = _L0_cond_setup()
    _L0_cond_in = {k: v for k, v in _L0_cond_all.items() if k in ('norm1_w', 'film1_w', 'film1_b', 'q_w', 'q_b', 'k_w', 'k_b', 'v_w', 'v_b', 'proj_w', 'proj_b', 'norm2_w', 'film2_w', 'film2_b', 'mlp_w1', 'mlp_b1', 'mlp_w2', 'mlp_b2')}
    del _L0_cond_all

    def _L1_cond_setup():
        import jax, jax.numpy as jnp
        import numpy as np
        EPS = 1e-06

        def _ln(x):
            m = jnp.mean(x, axis=-1, keepdims=True)
            v = jnp.mean(jnp.square(x - m), axis=-1, keepdims=True)
            return (x - m) * jax.lax.rsqrt(v + EPS)

        def _modulate(x, shift, scale):
            return x * (1.0 + scale[:, None]) + shift[:, None]
        key = jax.random.key(seed)
        B, S, H, NH = (8, 256, 256, 16)
        ks = jax.random.split(key, 12)
        s = lambda k, sh: jax.random.normal(k, sh, dtype=jnp.float32) * 0.02
        return {'x': jax.random.normal(ks[0], (B, S, H), dtype=jnp.float32), 'c': jax.random.normal(ks[1], (B, H), dtype=jnp.float32), 'w_ada': s(ks[2], (H, 6 * H)), 'b_ada': jnp.zeros((6 * H,), dtype=jnp.float32), 'w_qkv': s(ks[3], (H, 3 * H)), 'w_proj': s(ks[4], (H, H)), 'b_proj': jnp.zeros((H,), dtype=jnp.float32), 'w_mlp1': s(ks[5], (H, 4 * H)), 'b_mlp1': jnp.zeros((4 * H,), dtype=jnp.float32), 'w_mlp2': s(ks[6], (4 * H, H)), 'b_mlp2': jnp.zeros((H,), dtype=jnp.float32)}
    _L1_cond_all = _L1_cond_setup()
    _L1_cond_in = {k: v for k, v in _L1_cond_all.items() if k in ('w_ada', 'b_ada', 'w_qkv', 'w_proj', 'b_proj', 'w_mlp1', 'b_mlp1', 'w_mlp2', 'b_mlp2')}
    del _L1_cond_all
    return {'x': x, 'cond_1024': cond_1024, 'L0_cond_norm1_w': _L0_cond_in['norm1_w'], 'L0_cond_film1_w': _L0_cond_in['film1_w'], 'L0_cond_film1_b': _L0_cond_in['film1_b'], 'L0_cond_q_w': _L0_cond_in['q_w'], 'L0_cond_q_b': _L0_cond_in['q_b'], 'L0_cond_k_w': _L0_cond_in['k_w'], 'L0_cond_k_b': _L0_cond_in['k_b'], 'L0_cond_v_w': _L0_cond_in['v_w'], 'L0_cond_v_b': _L0_cond_in['v_b'], 'L0_cond_proj_w': _L0_cond_in['proj_w'], 'L0_cond_proj_b': _L0_cond_in['proj_b'], 'L0_cond_norm2_w': _L0_cond_in['norm2_w'], 'L0_cond_film2_w': _L0_cond_in['film2_w'], 'L0_cond_film2_b': _L0_cond_in['film2_b'], 'L0_cond_mlp_w1': _L0_cond_in['mlp_w1'], 'L0_cond_mlp_b1': _L0_cond_in['mlp_b1'], 'L0_cond_mlp_w2': _L0_cond_in['mlp_w2'], 'L0_cond_mlp_b2': _L0_cond_in['mlp_b2'], 'L1_cond_w_ada': _L1_cond_in['w_ada'], 'L1_cond_b_ada': _L1_cond_in['b_ada'], 'L1_cond_w_qkv': _L1_cond_in['w_qkv'], 'L1_cond_w_proj': _L1_cond_in['w_proj'], 'L1_cond_b_proj': _L1_cond_in['b_proj'], 'L1_cond_w_mlp1': _L1_cond_in['w_mlp1'], 'L1_cond_b_mlp1': _L1_cond_in['b_mlp1'], 'L1_cond_w_mlp2': _L1_cond_in['w_mlp2'], 'L1_cond_b_mlp2': _L1_cond_in['b_mlp2']}

def reference(x, cond_1024, L0_cond_norm1_w, L0_cond_film1_w, L0_cond_film1_b, L0_cond_q_w, L0_cond_q_b, L0_cond_k_w, L0_cond_k_b, L0_cond_v_w, L0_cond_v_b, L0_cond_proj_w, L0_cond_proj_b, L0_cond_norm2_w, L0_cond_film2_w, L0_cond_film2_b, L0_cond_mlp_w1, L0_cond_mlp_b1, L0_cond_mlp_w2, L0_cond_mlp_b2, L1_cond_w_ada, L1_cond_b_ada, L1_cond_w_qkv, L1_cond_w_proj, L1_cond_b_proj, L1_cond_w_mlp1, L1_cond_b_mlp1, L1_cond_w_mlp2, L1_cond_b_mlp2):
    import jax
    import jax.numpy as jnp

    def _L0_cond_ref(x, cond, norm1_w, film1_w, film1_b, q_w, q_b, k_w, k_b, v_w, v_b, proj_w, proj_b, norm2_w, film2_w, film2_b, mlp_w1, mlp_b1, mlp_w2, mlp_b2):
        import jax, jax.numpy as jnp
        import numpy as np
        DIM = 256
        MLP_RATIO = 4
        EPS = 1e-06

        def rmsnorm(x, w):
            return x * jax.lax.rsqrt(jnp.mean(x * x, axis=-1, keepdims=True) + EPS) * w

        def film(x, cond, w, b):
            ss = cond @ w + b
            scale, shift = jnp.split(ss, 2, axis=-1)
            return x * (1.0 + scale[:, None, :]) + shift[:, None, :]
        B, N, D = x.shape
        x_in = x
        h = film(rmsnorm(x, norm1_w), cond, film1_w, film1_b)
        Q = h @ q_w + q_b
        K = h @ k_w + k_b
        V = h @ v_w + v_b
        scores = jnp.einsum('bnd,bmd->bnm', Q, K) * D ** (-0.5)
        attn = jax.nn.softmax(scores, axis=-1)
        out = jnp.einsum('bnm,bmd->bnd', attn, V)
        x = x_in + (out @ proj_w + proj_b)
        x_in = x
        h = film(rmsnorm(x, norm2_w), cond, film2_w, film2_b)
        h = jax.nn.gelu(h @ mlp_w1 + mlp_b1, approximate=False) @ mlp_w2 + mlp_b2
        return x_in + h

    def _L1_cond_ref(x, c, w_ada, b_ada, w_qkv, w_proj, b_proj, w_mlp1, b_mlp1, w_mlp2, b_mlp2):
        import jax, jax.numpy as jnp
        import numpy as np
        EPS = 1e-06

        def _ln(x):
            m = jnp.mean(x, axis=-1, keepdims=True)
            v = jnp.mean(jnp.square(x - m), axis=-1, keepdims=True)
            return (x - m) * jax.lax.rsqrt(v + EPS)

        def _modulate(x, shift, scale):
            return x * (1.0 + scale[:, None]) + shift[:, None]
        B, S, H = x.shape
        NH = 16
        CH = H // NH
        cmod = jax.nn.silu(c) @ w_ada + b_ada
        shift_msa, scale_msa, gate_msa, shift_mlp, scale_mlp, gate_mlp = jnp.split(cmod, 6, axis=-1)
        x_mod = _modulate(_ln(x), shift_msa, scale_msa)
        qkv = x_mod @ w_qkv
        k, q, v = jnp.split(qkv, 3, axis=-1)
        k = k.reshape(B, S, NH, CH)
        q = q.reshape(B, S, NH, CH)
        v = v.reshape(B, S, NH, CH)
        q = q / CH
        w = jnp.einsum('bqhc,bkhc->bhqk', q, k).astype(jnp.float32)
        w = jax.nn.softmax(w, axis=-1)
        y = jnp.einsum('bhqk,bkhc->bqhc', w, v).reshape(B, S, H)
        attn_x = y @ w_proj + b_proj
        x = x + gate_msa[:, None] * attn_x
        x_mod2 = _modulate(_ln(x), shift_mlp, scale_mlp)
        h = jax.nn.gelu(x_mod2 @ w_mlp1 + b_mlp1)
        mlp_x = h @ w_mlp2 + b_mlp2
        x = x + gate_mlp[:, None] * mlp_x
        return x
    x = _L0_cond_ref(x, cond_1024, L0_cond_norm1_w, L0_cond_film1_w, L0_cond_film1_b, L0_cond_q_w, L0_cond_q_b, L0_cond_k_w, L0_cond_k_b, L0_cond_v_w, L0_cond_v_b, L0_cond_proj_w, L0_cond_proj_b, L0_cond_norm2_w, L0_cond_film2_w, L0_cond_film2_b, L0_cond_mlp_w1, L0_cond_mlp_b1, L0_cond_mlp_w2, L0_cond_mlp_b2)
    x = _L1_cond_ref(x, cond_1024, L1_cond_w_ada, L1_cond_b_ada, L1_cond_w_qkv, L1_cond_w_proj, L1_cond_b_proj, L1_cond_w_mlp1, L1_cond_b_mlp1, L1_cond_w_mlp2, L1_cond_b_mlp2)
    return x

_drawn_inputs = setup_inputs


def setup_inputs(seed=0):
    import zlib

    import numpy as np

    out = dict(_drawn_inputs(seed))
    spreads = {'L0_cond_norm1_w': (1.0, 0.2),
     'L0_cond_film1_b': (0.0, 0.1),
     'L0_cond_q_b': (0.0, 0.348),
     'L0_cond_k_b': (0.0, 2.0),
     'L0_cond_v_b': (0.0, 0.1),
     'L0_cond_proj_b': (0.0, 0.1),
     'L0_cond_norm2_w': (1.0, 0.2),
     'L0_cond_film2_b': (0.0, 0.1),
     'L0_cond_mlp_b1': (0.0, 0.1),
     'L0_cond_mlp_b2': (0.0, 0.1),
     'L1_cond_b_ada': (0.0, 0.8),
     'L1_cond_b_proj': (0.0, 0.723),
     'L1_cond_b_mlp1': (0.0, 0.8),
     'L1_cond_b_mlp2': (0.0, 0.788)}
    factors = {'L1_cond_w_ada': 2.84,
     'L1_cond_w_qkv': 6.452,
     'L1_cond_w_proj': 6.412,
     'L1_cond_w_mlp1': 4.553,
     'L1_cond_w_mlp2': 4.214}
    for name, (base, spread) in spreads.items():
        noise = np.random.default_rng([zlib.crc32(name.encode()), seed]).standard_normal(out[name].shape)
        drawn = base * np.exp(spread * noise) if base else spread * noise
        out[name] = jnp.asarray(drawn.astype(out[name].dtype))
    for name, factor in factors.items():
        out[name] = (out[name] * factor).astype(out[name].dtype)
    return out
```

```python
from contextlib import ExitStack

import concourse.bass as bass
from concourse import mybir
from concourse.alu_op_type import AluOpType as ALU

F32 = mybir.dt.float32
F32R = mybir.dt.float32r
ACT = mybir.ActivationFunctionType
AX = mybir.AxisListType.X

P = 128
EPS = 1e-6
UNROLL = 2
PEEL = 4


class Seq:

    def __init__(self, reg, off):
        self.reg, self.off = reg, off

    def back(self, n):
        return Seq(self.reg, self.off - n)

    @property
    def par(self):
        return self.off % UNROLL

    @property
    def num(self):
        return self.off if self.reg is None else self.reg * UNROLL + self.off

    @property
    def pair(self):
        return self.off // UNROLL if self.reg is None else self.reg + self.off // UNROLL

    def before_first(self):
        return self.reg is None and self.off < 0

    def exists(self, n):
        return self.reg is not None or 0 <= self.off < n


class Event:

    def __init__(self, sem, per, base=0):
        self.sem, self.per, self.base = sem, per, base

    def by(self, instruction):
        instruction.then_inc(self.sem, 1)

    def wait(self, eng, seq, k=None):
        k = self.per if k is None else k
        if seq.reg is not None or seq.off * self.per + k > 0:
            eng.wait_ge(self.sem, seq.num * self.per + self.base + k)


def run_pipeline(eng, n_seq, max_skew, iteration):
    for i in range(PEEL):
        iteration(Seq(None, i))
    with eng.Fori(PEEL // UNROLL, n_seq // UNROLL) as j:
        for u in range(UNROLL):
            iteration(Seq(j, u))
    for i in range(n_seq, n_seq + max_skew):
        iteration(Seq(None, i))


def build(nc, a, out, mod_dram):
    NB, S, D = a["x"].shape
    TH, KT = S // P, D // P
    HID = a["L0_cond_mlp_w1"].shape[1]
    HT = HID // P
    NH, CH = 16, D // 16
    assert TH == 2 and KT == 2 and HT == 8 and NB % UNROLL == 0

    root, semaphores, events = ExitStack(), ExitStack(), {}

    def allocator(stack, prefix):
        def sb(name, shape, dt=F32):
            return stack.enter_context(nc.sbuf_tensor(prefix + name, shape, dt))

        def ps(name, shape, dt=F32):
            return stack.enter_context(nc.psum_tensor(prefix + name, shape, dt))

        def sem(name):
            return semaphores.enter_context(nc.semaphore(prefix + name))

        def event(name, per=1):
            if name in events:
                old = events[name]
                assert old.per == per
                events[name] = Event(old.sem, per, old.base + NB * per)
            else:
                events[name] = Event(semaphores.enter_context(nc.semaphore("e_" + name)), per)
            return events[name]
        return sb, ps, sem, event

    with semaphores, root:
        sb, ps, sem, event = allocator(root, "")
        xres = sb("xres", [P, NB * TH * D])
        xv = xres[:, :].rearrange("p (j u h n) -> p j u h n", u=UNROLL, h=TH, n=D)
        ident = sb("ident", [P, P])
        banks = [ps(f"bank{i}", [P, 512]) for i in range(8)]
        neghalf = sb("neghalf", [P, TH])
        scale0a, shift0a = sb("scale0a", [P, KT * NB]), sb("shift0a", [P, KT * NB])
        scale0m, shift0m = sb("scale0m", [P, KT * NB]), sb("shift0m", [P, KT * NB])
        scale1a, shift1a = sb("scale1a", [P, KT * NB]), sb("shift1a", [P, KT * NB])
        scale1m, shift1m = sb("scale1m", [P, KT * NB]), sb("shift1m", [P, KT * NB])
        gates = sb("gates", [NB, 2 * D])

        def x_at(seq):
            return xv[:, seq.pair, seq.par]

        def per_seq(t, tile, seq):
            v = t[:, :].rearrange("p (t j u) -> p t j u", j=NB // UNROLL, u=UNROLL)
            return v[:, tile, seq.pair, seq.par:seq.par + 1]

        def mm3(eng, out_ap, pairs, start=True, stop=True, skip=False):
            last = None
            n = len(pairs)
            for i, ((a_hi, a_lo), (b_hi, b_lo)) in enumerate(pairs):
                for k, (l, r) in enumerate(((a_lo, b_hi), (a_hi, b_lo), (a_hi, b_hi))):
                    last = eng.matmul(out_ap, l, r, start=start and i == 0 and k == 0,
                                      stop=stop and i == n - 1 and k == 2, skip_group_check=skip)
            return last

        with ExitStack() as st:
            sb, ps, sem, event = allocator(st, "su_")
            cond = sb("cond", [NB, D])
            condT = sb("condT", [P, KT * NB])
            actT = sb("actT", [P, KT * NB])
            esig = sb("esig", [P, KT * NB])
            w_film1, w_film2 = sb("w_film1", [P, KT * 2 * D]), sb("w_film2", [P, KT * 2 * D])
            w_ada = sb("w_ada", [P, KT * 6 * D])
            b_film1, b_film2 = sb("b_film1", [P, 4]), sb("b_film2", [P, 4])
            b_ada = sb("b_ada", [P, 12])
            n1, n2 = sb("n1", [P, KT]), sb("n2", [P, KT])
            b_gate = sb("b_gate", [NB, 2 * D])
            pT, pmod, pgate = banks[:3]
            s_small, s_f1, s_f2, s_ada, s_x = (sem(n) for n in ("small", "f1", "f2", "ada", "x"))
            s_id, s_T, s_cT, s_e, s_act, s_mod, s_gate, s_fix = (
                sem(n) for n in ("id", "T", "cT", "e", "act", "mod", "gate", "fix"))

            def row(v, lo, n):
                return v[lo:lo + n]

            with nc.Block() as blk:
                @blk.sync
                def _(eng):
                    eng.dma_start(cond[:, :], a["cond_1024"]).then_inc(s_small, 16)
                    for w, d, s in ((w_film1, "L0_cond_film1_w", s_f1), (w_film2, "L0_cond_film2_w", s_f2),
                                    (w_ada, "L1_cond_w_ada", s_ada)):
                        eng.dma_start(w[:, :].rearrange("p (t n) -> p t n", t=KT),
                                      a[d].rearrange("(t p) n -> p t n", p=P)).then_inc(s, 16)
                    xd = a["x"].rearrange("b (h p) n -> p (b h) n", p=P)
                    xs = xres[:, :].rearrange("p (t n) -> p t n", n=D)
                    step = NB * TH // 4
                    for c in range(4):
                        eng.dma_start(xs[:, c * step:(c + 1) * step], xd[:, c * step:(c + 1) * step]).then_inc(s_x, 16)
                    eng.wait_ge(s_x, 16 * 4)

                @blk.gpsimd
                def _(eng):
                    eng.memset(neghalf[:, :], -0.5)
                    eng.memset(ident[:, :], 0.0).then_inc(s_id, 1)
                    eng.wait_ge(s_id, 1)
                    eng.affine_select(out=ident[:, :], in_=ident[:, :], compare_op=ALU.not_equal, fill=1.0,
                                      base=0, pattern=[[-1, P]], channel_multiplier=1).then_inc(s_id, 1)

                @blk.scalar
                def _(eng):
                    with nc.allow_non_contiguous_dma(reason="bias vectors, one element per partition"):
                        for t, v in ((b_film1, a["L0_cond_film1_b"]), (b_film2, a["L0_cond_film2_b"]),
                                     (b_ada, a["L1_cond_b_ada"]), (n1, a["L0_cond_norm1_w"]),
                                     (n2, a["L0_cond_norm2_w"])):
                            eng.dma_start(t[:, :], v.rearrange("(t p) -> p t", p=P)).then_inc(s_small, 16)
                    for g, lo in enumerate((2 * D, 5 * D)):
                        eng.dma_start(b_gate[:, g * D:(g + 1) * D],
                                      row(a["L1_cond_b_ada"], lo, D).partition_broadcast(NB)).then_inc(s_small, 16)
                    eng.wait_ge(s_cT, 1)
                    eng.activation(esig[:, :], condT[:, :], ACT.Exp, scale=-1.0).then_inc(s_e, 1)

                @blk.tensor
                def _(eng):
                    eng.wait_ge(s_small, 16 * 8)
                    eng.wait_ge(s_id, 2)
                    for t in range(KT):
                        m = eng.transpose(pT[:, t * NB:(t + 1) * NB], cond[:, t * P:(t + 1) * P], ident[0:NB, 0:NB])
                    m.then_inc(s_T, 1)
                    slot = 0
                    eng.wait_ge(s_cT, 1)
                    for w, s, rhs, cols, width in (
                            (w_film1, s_f1, condT, range(4), 2 * D), (w_film2, s_f2, condT, range(4), 2 * D),
                            (w_ada, s_ada, actT, (0, 1, 2, 3, 6, 7, 8, 9), 6 * D)):
                        eng.wait_ge(s, 16)
                        if rhs is actT:
                            eng.wait_ge(s_act, 1)
                        for c in cols:
                            for t in range(KT):
                                m = eng.matmul(pmod[:, slot * NB:(slot + 1) * NB],
                                               w[:, t * width + c * P:t * width + (c + 1) * P],
                                               rhs[:, t * NB:(t + 1) * NB], start=t == 0, stop=t == KT - 1)
                            slot += 1
                    m.then_inc(s_mod, 1)
                    for g, lo in enumerate((2 * D, 5 * D)):
                        for t in range(KT):
                            m = eng.matmul(pgate[0:NB, g * D:(g + 1) * D], actT[:, t * NB:(t + 1) * NB],
                                           w_ada[:, t * 6 * D + lo:t * 6 * D + lo + D], start=t == 0, stop=t == KT - 1)
                    m.then_inc(s_gate, 1)

                @blk.vector
                def _(eng):
                    eng.wait_ge(s_T, 1)
                    eng.tensor_copy(condT[:, :], pT[:, 0:KT * NB]).then_inc(s_cT, 1)
                    eng.wait_ge(s_e, 1)
                    eng.tensor_scalar(esig[:, :], esig[:, :], 1.0, None, ALU.add).then_inc(s_fix, 1)
                    eng.wait_ge(s_fix, 1)
                    eng.reciprocal(actT[:, :], esig[:, :]).then_inc(s_fix, 1)
                    eng.wait_ge(s_fix, 2)
                    eng.tensor_tensor(actT[:, :], actT[:, :], condT[:, :], ALU.mult).then_inc(s_act, 1)
                    eng.wait_ge(s_small, 16 * 8)
                    for b, lo, n in ((b_film1, 0, 2), (b_film2, 0, 2), (b_ada, 2, 2), (b_ada, 8, 2)):
                        eng.tensor_scalar(b[:, lo:lo + n], b[:, lo:lo + n], 1.0, None, ALU.add).then_inc(s_fix, 1)
                    eng.wait_ge(s_fix, 6)
                    eng.wait_ge(s_mod, 1)
                    slot = 0
                    for dst, b, lo, norm in ((scale0a, b_film1, 0, n1), (shift0a, b_film1, 2, None),
                                             (scale0m, b_film2, 0, n2), (shift0m, b_film2, 2, None),
                                             (shift1a, b_ada, 0, None), (scale1a, b_ada, 2, None),
                                             (shift1m, b_ada, 6, None), (scale1m, b_ada, 8, None)):
                        for t in range(KT):
                            src = pmod[:, slot * NB:(slot + 1) * NB]
                            o = dst[:, t * NB:(t + 1) * NB]
                            if norm is None:
                                eng.tensor_scalar(o, src, b[:, lo + t:lo + t + 1], None, ALU.add)
                            else:
                                eng.tensor_scalar(o, src, b[:, lo + t:lo + t + 1], norm[:, t:t + 1], ALU.add, ALU.mult)
                            slot += 1
                    eng.wait_ge(s_gate, 1)
                    eng.tensor_tensor(gates[:, :], pgate[0:NB, :], b_gate[:, :], ALU.add)

        class Norm:

            def __init__(self, sb, event, rms, scale, bank, reader):
                self.rms, self.scale, self.bank, self.reader = rms, scale, bank, reader
                self.stat = sb("stat", [P, TH * 6])
                self.mv = sb("mv", [P, TH * 2])
                self.var = sb("var", [P, TH])
                self.msq = sb("msq", [P, TH])
                self.rstd = sb("rstd", [P, TH])
                self.xhat = sb("xhat", [P, TH * D])
                self.hi = [sb(f"h_hi{u}", [P, KT * S], F32R) for u in range(UNROLL)]
                self.lo = [sb(f"h_lo{u}", [P, KT * S], F32R) for u in range(UNROLL)]
                self.e_mv = event("mv")
                self.e_msq = event("msq") if rms else None
                self.e_var = event("var")
                self.e_rstd = event("rstd")
                self.e_xhat = event("xhat")
                self.e_T = event("T")
                self.e_hi = event("hhi")
                self.e_lo = event("hlo")

            def stats(self, eng, b):
                mv = self.mv[:, :].rearrange("p (h c) -> p h c", c=2)
                self.e_rstd.wait(eng, b.back(1))
                self.e_xhat.wait(eng, b.back(1))
                for h in range(TH):
                    eng.bn_stats(self.stat[:, 6 * h:6 * h + 6], x_at(b)[:, h])
                eng.drain()
                for h in range(TH):
                    ins = eng.bn_aggr(self.mv[:, 2 * h:2 * h + 2], self.stat[:, 6 * h:6 * h + 6])
                self.e_mv.by(ins)
                self.e_mv.wait(eng, b)
                if self.rms:
                    self.e_msq.by(eng.tensor_tensor(self.msq[:, :], mv[:, :, 0], mv[:, :, 0], ALU.mult))
                    self.e_msq.wait(eng, b)
                    ins = eng.scalar_tensor_tensor(out=self.var[:, :], in0=self.msq[:, :], scalar=EPS,
                                                   in1=mv[:, :, 1], op0=ALU.add, op1=ALU.add)
                else:
                    ins = eng.tensor_scalar(self.var[:, :], mv[:, :, 1], EPS, None, ALU.add)
                self.e_var.by(ins)

            def root(self, eng, b):
                self.e_var.wait(eng, b)
                self.e_xhat.wait(eng, b.back(1))
                self.e_rstd.by(eng.tensor_tensor(self.rstd[:, :], self.var[:, :], neghalf[:, :], ALU.pow))

            def normalize(self, eng, b):
                self.e_rstd.wait(eng, b)
                self.e_T.wait(eng, b.back(1))
                for h in range(TH):
                    r = self.rstd[:, h:h + 1]
                    o = self.xhat[:, h * D:(h + 1) * D]
                    if self.rms:
                        ins = eng.tensor_scalar(o, x_at(b)[:, h], r, None, ALU.mult)
                    else:
                        ins = eng.tensor_scalar(o, x_at(b)[:, h], self.mv[:, 2 * h:2 * h + 1], r,
                                                ALU.subtract, ALU.mult)
                self.e_xhat.by(ins)

            def transpose(self, eng, b):
                self.e_xhat.wait(eng, b)
                for t in range(KT):
                    for h in range(TH):
                        ins = eng.transpose(self.bank[:, t * S + h * P:t * S + (h + 1) * P],
                                            self.xhat[:, h * D + t * P:h * D + (t + 1) * P], ident[:, :])
                self.e_T.by(ins)

            def evac_hi(self, eng, b):
                self.e_T.wait(eng, b)
                ev, k = self.reader
                ev.wait(eng, b.back(UNROLL), k)
                for t in range(KT):
                    ins = eng.activation(self.hi[b.par][:, t * S:(t + 1) * S], self.bank[:, t * S:(t + 1) * S],
                                         ACT.Copy, scale=per_seq(self.scale, t, b))
                self.e_hi.by(ins)

            def evac_lo(self, eng, b):
                self.e_hi.wait(eng, b)
                for t in range(KT):
                    c = slice(t * S, (t + 1) * S)
                    ins = eng.scalar_tensor_tensor(out=self.lo[b.par][:, c], in0=self.bank[:, c],
                                                   scalar=per_seq(self.scale, t, b),
                                                   in1=self.hi[b.par][:, c].bitcast(F32),
                                                   op0=ALU.mult, op1=ALU.subtract)
                self.e_lo.by(ins)

            def tokens(self, b, t, h=None):
                c = slice(t * S, (t + 1) * S) if h is None else slice(t * S + h * P, t * S + (h + 1) * P)
                return self.hi[b.par][:, c], self.lo[b.par][:, c]

        def hold_weights(sb, specs):
            return {key: (sb("wt_" + key + "_hi", [P, v.shape[0] // P * v.shape[1]], F32R),
                          sb("wt_" + key + "_lo", [P, v.shape[0] // P * v.shape[1]], F32R), v) for key, v in specs}

        def load_weights(sb, sem, held):
            return {key: (sb("wt_" + key + "_raw", [P, v.shape[0] // P * v.shape[1]]), hi, lo, v.shape[0] // P, v.shape[1],
                          v, sem(key + "_in"), sem(key + "_sp")) for key, (hi, lo, v) in held.items()}

        def emit_loads(eng, ws):
            for raw, hi, lo, t, N, view, s_in, s_sp in ws.values():
                eng.dma_start(raw[:, :].rearrange("p (t n) -> p t n", t=t),
                              view.rearrange("(t p) n -> p t n", p=P)).then_inc(s_in, 16)

        def emit_hi(eng, ws):
            for raw, hi, lo, t, N, view, s_in, s_sp in ws.values():
                eng.wait_ge(s_in, 16)
                eng.activation(hi[:, :], raw[:, :], ACT.Copy).then_inc(s_sp, 1)

        def emit_lo(eng, ws):
            for raw, hi, lo, t, N, view, s_in, s_sp in ws.values():
                eng.wait_ge(s_sp, 1)
                eng.tensor_tensor(lo[:, :], raw[:, :], hi[:, :].bitcast(F32), ALU.subtract)

        def shift_bias(eng, psum, col, w, c0, shift):
            raw, _, _, t, N, _, s_in, _ = w
            eng.wait_ge(s_in, 16)
            for k in range(KT):
                ins = eng.matmul(psum[:, col:col + NB], raw[:, k * N + c0:k * N + c0 + P],
                                 shift[:, k * NB:(k + 1) * NB], start=k == 0, stop=k == KT - 1)
            return ins

        def weight(w, k, c0, n):
            _, hi, lo, t, N, *_ = w
            return hi[:, k * N + c0:k * N + c0 + n], lo[:, k * N + c0:k * N + c0 + n]

        def phase_l0_attention():
            with ExitStack() as st:
                sb, ps, sem, event = allocator(st, "A_")
                bT, bQ, bK, bV, bS, bPT, bR = banks[:7]
                biasq, biask = (sb(n, [P, KT * NB]) for n in ("biasq", "biask"))
                held = hold_weights(sb, [(k, a[f"L0_cond_{k}_w"]) for k in ("q", "k")])
                vp_hi, vp_lo = sb("vp_hi", [P, KT * D], F32R), sb("vp_lo", [P, KT * D], F32R)
                with ExitStack() as pre:
                    psb, _, psem, _ = allocator(pre, "Ap_")
                    ws = load_weights(psb, psem, held)
                    w_v, w_p, w_vT, w_vp = (psb(n, [P, KT * D]) for n in ("w_v", "w_p", "w_vT", "w_vp"))
                    biaso = psb("biaso", [P, KT * NB])
                    orow = psb("orow", [NB, D])
                    bcol = [psb(n, [P, KT]) for n in ("bq", "bk", "bv")]
                    s_b, s_mm, s_vp, s_vT, s_vpm, s_cp, s_row = (psem(n) for n in ("b", "mm", "vp", "vT", "vpm", "cp", "row"))
                    pT, pvp, prow = banks[1], banks[2], banks[3]
                    with nc.Block() as blk:
                        @blk.sync
                        def _(eng):
                            emit_loads(eng, ws)
                            for w, k in ((w_v, "v"), (w_p, "proj")):
                                eng.dma_start(w[:, :].rearrange("p (t n) -> p t n", t=KT),
                                              a[f"L0_cond_{k}_w"].rearrange("(t p) n -> p t n", p=P)).then_inc(s_vp, 16)
                            with nc.allow_non_contiguous_dma(reason="bias vectors, one element per partition"):
                                for t, k in zip(bcol, "qkv"):
                                    eng.dma_start(t[:, :], a[f"L0_cond_{k}_b"].rearrange("(t p) -> p t", p=P)).then_inc(s_b, 16)
                            eng.dma_start(orow[:, :], a["L0_cond_proj_b"].partition_broadcast(NB)).then_inc(s_b, 16)
                            eng.wait_ge(s_row, 2)
                            eng.dma_start(mod_dram[2, :, 0:D], orow[:, :]).then_inc(s_row, 16)
                            eng.wait_ge(s_row, 2 + 16)

                        @blk.scalar
                        def _(eng):
                            emit_hi(eng, ws)
                            eng.wait_ge(s_cp, 3)
                            eng.activation(vp_hi[:, :], w_vp[:, :], ACT.Copy).then_inc(s_cp, 1)

                        @blk.tensor
                        def _(eng):
                            eng.wait_ge(s_vp, 32)
                            for c in range(KT):
                                for r in range(KT):
                                    ins = eng.transpose(pT[:, c * D + r * P:c * D + (r + 1) * P],
                                                        w_v[:, r * D + c * P:r * D + (c + 1) * P], ident[:, :])
                            ins.then_inc(s_vT, 1)
                            for i, k in enumerate("qk"):
                                for t in range(KT):
                                    shift_bias(eng, banks[0], (i * KT + t) * NB, ws[k], t * P, shift0a)
                            for t in range(KT):
                                for k in range(KT):
                                    ins = eng.matmul(banks[0][:, (4 + t) * NB:(5 + t) * NB],
                                                     w_v[:, k * D + t * P:k * D + (t + 1) * P],
                                                     shift0a[:, k * NB:(k + 1) * NB], start=k == 0, stop=k == KT - 1)
                            ins.then_inc(s_mm, 1)
                            eng.wait_ge(s_cp, 1)
                            for r in range(KT):
                                for c in range(KT):
                                    ins = eng.matmul(pvp[:, r * D:(r + 1) * D], w_vT[:, c * D + r * P:c * D + (r + 1) * P],
                                                     w_p[:, c * D:(c + 1) * D], start=c == 0, stop=c == KT - 1)
                            ins.then_inc(s_vpm, 1)
                            eng.wait_ge(s_cp, 2)
                            for k in range(KT):
                                ins = eng.matmul(prow[0:NB, 0:D], biaso[:, k * NB:(k + 1) * NB], w_p[:, k * D:(k + 1) * D],
                                                 start=k == 0, stop=k == KT - 1)
                            ins.then_inc(s_row, 1)

                        @blk.vector
                        def _(eng):
                            eng.wait_ge(s_vT, 1)
                            eng.tensor_copy(w_vT[:, :], pT[:, :]).then_inc(s_cp, 1)
                            eng.wait_ge(s_b, 16 * 4)
                            eng.wait_ge(s_mm, 1)
                            for i, dst in enumerate((biasq, biask, biaso)):
                                for t in range(KT):
                                    c = (i * KT + t) * NB
                                    ins = eng.tensor_scalar(dst[:, t * NB:(t + 1) * NB], banks[0][:, c:c + NB],
                                                            bcol[i][:, t:t + 1], None, ALU.add)
                            ins.then_inc(s_cp, 1)
                            eng.wait_ge(s_vpm, 1)
                            eng.tensor_copy(w_vp[:, :], pvp[:, :]).then_inc(s_cp, 1)
                            eng.wait_ge(s_row, 1)
                            eng.tensor_tensor(orow[:, :], prow[0:NB, 0:D], orow[:, :], ALU.add).then_inc(s_row, 1)
                            emit_lo(eng, ws)
                            eng.wait_ge(s_cp, 4)
                            eng.tensor_tensor(vp_lo[:, :], w_vp[:, :], vp_hi[:, :].bitcast(F32), ALU.subtract)

                qk = {n: sb(n, [P, KT * S], F32R) for n in ("q_hi", "q_lo", "k_hi", "k_lo")}
                v_hi = [sb(f"v_hi{u}", [P, TH * D], F32R) for u in range(UNROLL)]
                v_lo = [sb(f"v_lo{u}", [P, TH * D], F32R) for u in range(UNROLL)]
                probs = sb("probs", [P, TH * S])
                negmax, negbias = sb("negmax", [P, TH]), sb("negbias", [P, TH])
                psums, prec = sb("psums", [P, TH]), sb("prec", [P, TH])
                pT_hi, pT_lo = sb("pT_hi", [P, TH * S], F32R), sb("pT_lo", [P, TH * S], F32R)
                orow_bc = [sb(f"orow_bc{u}", [P, D]) for u in range(UNROLL)]
                s_row = [sem(f"row{u}") for u in range(UNROLL)]
                xb = [sb(f"xb{u}", [P, TH * D]) for u in range(UNROLL)]
                e_q, e_k, e_v, e_s, e_pT, e_av = (event(n) for n in ("q", "k", "v", "s1", "pT", "av1"))
                e_hi = {n: event("hi_" + n) for n in ("q", "k", "v", "p")}
                e_lo = {n: event("lo_" + n) for n in ("q", "k", "v", "p")}
                e_max, e_nb, e_exp, e_rec, e_nrm = (event(n) for n in ("max1", "nb", "exp1", "rec", "nrm"))
                e_xb, e_res = event("xb"), event("res")
                norm = Norm(sb, event, True, scale0a, bT, (e_v, 1))
                scl = float(D) ** -0.5

                def hi_bias(eng, b, name, bk, dst, bias, e_in, e_reader):
                    e_in.wait(eng, b)
                    e_reader.wait(eng, b.back(1))
                    for t in range(KT):
                        c = slice(t * S, (t + 1) * S)
                        ins = eng.activation(dst[:, c], bk[:, c], ACT.Identity, bias=per_seq(bias, t, b))
                    e_hi[name].by(ins)

                def lo_bias(eng, b, name, bk, hi, lo, bias):
                    e_hi[name].wait(eng, b)
                    for t in range(KT):
                        c = slice(t * S, (t + 1) * S)
                        ins = eng.scalar_tensor_tensor(out=lo[:, c], in0=bk[:, c], scalar=per_seq(bias, t, b),
                                                       in1=hi[:, c].bitcast(F32), op0=ALU.add, op1=ALU.subtract)
                    e_lo[name].by(ins)

                def hi_plain(eng, b, name, bk, dst, e_in, e_reader, buffers=1):
                    e_in.wait(eng, b)
                    e_reader.wait(eng, b.back(buffers))
                    e_hi[name].by(eng.activation(dst[:, :], bk[:, :], ACT.Copy))

                def lo_plain(eng, b, name, bk, hi, lo):
                    e_hi[name].wait(eng, b)
                    e_lo[name].by(eng.tensor_tensor(lo[:, :], bk[:, :], hi[:, :].bitcast(F32), ALU.subtract))

                with nc.Block() as blk:
                    @blk.tensor
                    def _(eng):
                        def proj_cm(b, bk, w, free, done):
                            norm.e_lo.wait(eng, b)
                            free.wait(eng, b.back(1))
                            for t in range(KT):
                                ins = mm3(eng, bk[:, t * S:(t + 1) * S],
                                          [(weight(ws[w], k, t * P, P), norm.tokens(b, k)) for k in range(KT)])
                            done.by(ins)

                        def it(i):
                            f, m, r = i.back(1), i.back(2), i.back(3)
                            if m.exists(NB):
                                proj_cm(m, bQ, "q", e_lo["q"], e_q)
                                proj_cm(m, bK, "k", e_lo["k"], e_k)
                            if r.exists(NB):
                                e_nrm.wait(eng, r)
                                e_lo["p"].wait(eng, r.back(1))
                                for kh in range(TH):
                                    for qh in range(TH):
                                        ins = eng.transpose(bPT[:, kh * S + qh * P:kh * S + (qh + 1) * P],
                                                            probs[:, qh * S + kh * P:qh * S + (kh + 1) * P], ident[:, :])
                                e_pT.by(ins)
                            if m.exists(NB):
                                norm.e_lo.wait(eng, m)
                                e_lo["v"].wait(eng, m.back(1))
                                for h in range(TH):
                                    ins = mm3(eng, bV[:, h * D:(h + 1) * D],
                                              [(norm.tokens(m, k, h), (vp_hi[:, k * D:(k + 1) * D], vp_lo[:, k * D:(k + 1) * D]))
                                               for k in range(KT)])
                                e_v.by(ins)
                            if r.exists(NB):
                                e_lo["p"].wait(eng, r)
                                e_res.wait(eng, r.back(1))
                                for qh in range(TH):
                                    cols = [slice(kh * S + qh * P, kh * S + (qh + 1) * P) for kh in range(TH)]
                                    ins = mm3(eng, bR[:, qh * D:(qh + 1) * D], [
                                        ((pT_hi[:, cols[kh]], pT_lo[:, cols[kh]]),
                                         (v_hi[r.par][:, kh * D:(kh + 1) * D], v_lo[r.par][:, kh * D:(kh + 1) * D]))
                                        for kh in range(TH)])
                                e_av.by(ins)
                            if f.exists(NB):
                                norm.e_lo.wait(eng, f.back(1))
                                norm.transpose(eng, f)
                            if m.exists(NB):
                                e_lo["q"].wait(eng, m)
                                e_lo["k"].wait(eng, m)
                                e_exp.wait(eng, m.back(1))
                                for qh in range(TH):
                                    ins = mm3(eng, bS[:, qh * S:(qh + 1) * S], [
                                        ((qk["q_hi"][:, t * S + qh * P:t * S + (qh + 1) * P],
                                          qk["q_lo"][:, t * S + qh * P:t * S + (qh + 1) * P]),
                                         (qk["k_hi"][:, t * S:(t + 1) * S], qk["k_lo"][:, t * S:(t + 1) * S]))
                                        for t in range(KT)])
                                e_s.by(ins)
                        run_pipeline(eng, NB, 3, it)

                    @blk.scalar
                    def _(eng):
                        def it(i):
                            f, m, r = i.back(1), i.back(2), i.back(3)
                            if m.exists(NB):
                                hi_bias(eng, m, "q", bQ, qk["q_hi"], biasq, e_q, e_s)
                                hi_bias(eng, m, "k", bK, qk["k_hi"], biask, e_k, e_s)
                            if r.exists(NB):
                                hi_plain(eng, r, "p", bPT, pT_hi, e_pT, e_av)
                            if m.exists(NB):
                                hi_plain(eng, m, "v", bV, v_hi[m.par], e_v, e_av, UNROLL)
                            if f.exists(NB):
                                norm.evac_hi(eng, f)
                            if m.exists(NB):
                                e_nb.wait(eng, m)
                                e_pT.wait(eng, m.back(1))
                                e_rec.wait(eng, m.back(1))
                                for h in range(TH):
                                    ins = eng.activation(probs[:, h * S:(h + 1) * S], bS[:, h * S:(h + 1) * S], ACT.Exp,
                                                         bias=negbias[:, h:h + 1], scale=scl,
                                                         accum_out=psums[:, h:h + 1])
                                e_exp.by(ins)
                        run_pipeline(eng, NB, 3, it)

                    @blk.vector
                    def _(eng):
                        def it(i):
                            n, f, m, r = i, i.back(1), i.back(2), i.back(3)
                            if m.exists(NB):
                                lo_bias(eng, m, "q", bQ, qk["q_hi"], qk["q_lo"], biasq)
                            if n.exists(NB):
                                norm.stats(eng, n)
                            if m.exists(NB):
                                lo_bias(eng, m, "k", bK, qk["k_hi"], qk["k_lo"], biask)
                            if r.exists(NB):
                                lo_plain(eng, r, "p", bPT, pT_hi, pT_lo)
                            if m.exists(NB):
                                lo_plain(eng, m, "v", bV, v_hi[m.par], v_lo[m.par])
                            if f.exists(NB):
                                norm.evac_lo(eng, f)
                            if n.exists(NB):
                                norm.normalize(eng, n)
                            if m.exists(NB):
                                e_s.wait(eng, m)
                                e_nb.wait(eng, m.back(1))
                                e_max.by(eng.tensor_reduce(negmax[:, :],
                                                           bS[:, :].rearrange("p (h k) -> p h k", h=TH),
                                                           AX, ALU.max, negate=True))
                                e_max.wait(eng, m)
                                e_exp.wait(eng, m.back(1))
                                e_nb.by(eng.tensor_scalar(negbias[:, :], negmax[:, :], scl, None, ALU.mult))
                            if r.exists(NB):
                                e_av.wait(eng, r)
                                e_xb.wait(eng, r)
                                e_res.by(eng.tensor_tensor(x_at(r), bR[:, :].rearrange("p (h n) -> p h n", h=TH),
                                                           xb[r.par][:, :].rearrange("p (h n) -> p h n", h=TH), ALU.add))
                            if m.exists(NB):
                                e_exp.wait(eng, m)
                                e_nrm.wait(eng, m.back(1))
                                e_rec.by(eng.reciprocal(prec[:, :], psums[:, :]))
                                e_rec.wait(eng, m)
                                for h in range(TH):
                                    ins = eng.tensor_scalar(probs[:, h * S:(h + 1) * S], probs[:, h * S:(h + 1) * S],
                                                            prec[:, h:h + 1], None, ALU.mult)
                                e_nrm.by(ins)
                        run_pipeline(eng, NB, 3, it)

                    @blk.gpsimd
                    def _(eng):
                        def it(i):
                            if i.exists(NB):
                                norm.root(eng, i)
                            m = i.back(2)
                            if m.exists(NB):
                                e_res.wait(eng, m.back(UNROLL))
                                eng.wait_ge(s_row[m.par], (m.pair + 1) * 16)
                                for h in range(TH):
                                    ins = eng.tensor_tensor(xb[m.par][:, h * D:(h + 1) * D], x_at(m)[:, h],
                                                            orow_bc[m.par][:, :], ALU.add)
                                e_xb.by(ins)
                        run_pipeline(eng, NB, 3, it)

                    @blk.sync
                    def _(eng):
                        rd = mod_dram[2].rearrange("(j u) n -> j u n", u=UNROLL)

                        def it(i):
                            f = i.back(1)
                            if f.exists(NB):
                                e_xb.wait(eng, f.back(UNROLL))
                                eng.dma_start(orow_bc[f.par][:, :], rd[f.pair, f.par, 0:D].partition_broadcast(P))\
                                   .then_inc(s_row[f.par], 16)
                        run_pipeline(eng, NB, 3, it)

        def phase_mlp(layer):
            l1 = layer == 1
            with ExitStack() as st:
                sb, ps, sem, event = allocator(st, "BD"[layer] + "_")
                hbank, tbank, obank = banks[:4], banks[4], banks[5:7]
                bias1 = sb("bias1", [P, HT * NB])
                gate_row = sb("gate_row", [NB, 2 * D]) if l1 else None
                bias2 = None if l1 else sb("bias2", [P, D])
                w1n, w2n, b1n, b2n = (("L1_cond_w_mlp1", "L1_cond_w_mlp2", "L1_cond_b_mlp1", "L1_cond_b_mlp2") if l1 else
                                      ("L0_cond_mlp_w1", "L0_cond_mlp_w2", "L0_cond_mlp_b1", "L0_cond_mlp_b2"))
                held = hold_weights(sb, [("w1", a[w1n]), ("w2", a[w2n])])
                with ExitStack() as pre:
                    psb, _, psem, _ = allocator(pre, "BD"[layer] + "p_")
                    ws = load_weights(psb, psem, held)
                    bcol = psb("bcol", [P, HT])
                    b2row = psb("b2row", [NB, D]) if l1 else None
                    s_b, s_mm, s_g = psem("b"), psem("mm"), psem("g")
                    with nc.Block() as blk:
                        @blk.sync
                        def _(eng):
                            emit_loads(eng, ws)
                            with nc.allow_non_contiguous_dma(reason="bias vectors, one element per partition"):
                                eng.dma_start(bcol[:, :], a[b1n].rearrange("(t p) -> p t", p=P)).then_inc(s_b, 16)
                            if l1:
                                eng.dma_start(b2row[:, :], a[b2n].partition_broadcast(NB)).then_inc(s_b, 16)
                                eng.wait_ge(s_g, 2)
                                eng.dma_start(mod_dram[1], gate_row[:, :]).then_inc(s_b, 16)
                                eng.wait_ge(s_b, 48)
                            else:
                                eng.dma_start(bias2[:, :], a[b2n].partition_broadcast(P)).then_inc(s_b, 16)

                        @blk.scalar
                        def _(eng):
                            emit_hi(eng, ws)

                        @blk.tensor
                        def _(eng):
                            for t in range(HT):
                                ins = shift_bias(eng, hbank[0], t * NB, ws["w1"], t * P, shift1m if l1 else shift0m)
                            ins.then_inc(s_mm, 1)

                        @blk.vector
                        def _(eng):
                            if l1:
                                eng.wait_ge(s_b, 32)
                                eng.tensor_copy(gate_row[:, 0:D], gates[:, D:2 * D]).then_inc(s_g, 1)
                                eng.tensor_tensor(gate_row[:, D:2 * D], gates[:, D:2 * D], b2row[:, :], ALU.mult).then_inc(s_g, 1)
                            emit_lo(eng, ws)
                            eng.wait_ge(s_b, 32)
                            eng.wait_ge(s_mm, 1)
                            for t in range(HT):
                                eng.tensor_scalar(bias1[:, t * NB:(t + 1) * NB], hbank[0][:, t * NB:(t + 1) * NB],
                                                  bcol[:, t:t + 1], None, ALU.add)

                g = [sb(f"g{u}", [P, 2 * S]) for u in range(4)]
                g_hi = [sb(f"g_hi{u}", [P, 2 * S], F32R) for u in range(4)]
                g_lo = [sb(f"g_lo{u}", [P, 2 * S], F32R) for u in range(4)]
                xb = [sb(f"xb{u}", [P, TH * D]) for u in range(UNROLL)]
                gbc = [sb(f"gbc{u}", [P, 2 * D]) for u in range(UNROLL)] if l1 else None
                tmp = sb("tmp", [P, TH * D]) if l1 else None
                e_mm1, e_gelu, e_ghi, e_glo, e_mm2 = (event(n, 4) for n in ("mm1", "gelu", "ghi", "glo", "mm2"))
                e_res, e_xb = event("res"), event("xb")
                e_tmp = event("tmp") if l1 else None
                s_gin = [sem(f"gin{u}") for u in range(UNROLL)]
                s_out = [sem(f"out{u}") for u in range(UNROLL)]
                norm = Norm(sb, event, not l1, scale1m if l1 else scale0m, tbank, (e_mm1, 4))
                func = ACT.Gelu_apprx_tanh if l1 else ACT.Gelu

                with nc.Block() as blk:
                    @blk.tensor
                    def _(eng):
                        def up(b, u):
                            if not b.exists(NB):
                                return
                            if u == 0:
                                norm.e_lo.wait(eng, b)
                            e_gelu.wait(eng, b.back(1), u + 1)
                            for d in range(2):
                                ins = mm3(eng, hbank[u][:, d * S:(d + 1) * S],
                                          [(weight(ws["w1"], k, (2 * u + d) * P, P), norm.tokens(b, k)) for k in range(KT)])
                            e_mm1.by(ins)

                        def down(b, u):
                            if not b.exists(NB):
                                return
                            e_glo.wait(eng, b, u + 1)
                            if u == 0:
                                e_res.wait(eng, b.back(UNROLL))
                            for h in range(TH):
                                for d in range(2):
                                    c = slice(d * S + h * P, d * S + (h + 1) * P)
                                    ins = mm3(eng, obank[b.par][:, h * D:(h + 1) * D],
                                              [((g_hi[u][:, c], g_lo[u][:, c]), weight(ws["w2"], 2 * u + d, 0, D))],
                                              start=u == 0 and h == 0 and d == 0, stop=u == 3 and d == 1, skip=True)
                            e_mm2.by(ins)

                        def it(i):
                            f, m, r = i, i.back(1), i.back(2)
                            up(m, 0)
                            down(r, 3)
                            up(m, 1)
                            down(m, 0)
                            up(m, 2)
                            down(m, 1)
                            if f.exists(NB):
                                norm.e_lo.wait(eng, f.back(1))
                                norm.transpose(eng, f)
                            up(m, 3)
                            down(m, 2)
                        run_pipeline(eng, NB, 2, it)

                    @blk.scalar
                    def _(eng):
                        def gelu(b, u):
                            if not b.exists(NB):
                                return
                            e_mm1.wait(eng, b, u + 1)
                            e_glo.wait(eng, b.back(1), u + 1)
                            for d in range(2):
                                ins = eng.activation(g[u][:, d * S:(d + 1) * S], hbank[u][:, d * S:(d + 1) * S], func,
                                                     bias=per_seq(bias1, 2 * u + d, b))
                            e_gelu.by(ins)

                        def it(i):
                            f, m = i, i.back(1)
                            for u in range(3):
                                gelu(m, u)
                            if f.exists(NB):
                                norm.evac_hi(eng, f)
                            gelu(m, 3)
                        run_pipeline(eng, NB, 2, it)

                    @blk.vector
                    def _(eng):
                        def split(b, u):
                            if not b.exists(NB):
                                return
                            e_gelu.wait(eng, b, u + 1)
                            e_mm2.wait(eng, b.back(1), u + 1)
                            e_ghi.by(eng.tensor_copy(g_hi[u][:, :], g[u][:, :]))
                            e_ghi.wait(eng, b, u + 1)
                            e_glo.by(eng.tensor_tensor(g_lo[u][:, :], g[u][:, :], g_hi[u][:, :].bitcast(F32), ALU.subtract))

                        def it(i):
                            f, m, r = i, i.back(1), i.back(2)
                            if f.exists(NB):
                                norm.stats(eng, f)
                            split(m, 0)
                            if r.exists(NB):
                                e_mm2.wait(eng, r)
                                e_xb.wait(eng, r)
                                o3 = obank[r.par][:, :].rearrange("p (h n) -> p h n", h=TH)
                                x3 = xb[r.par][:, :].rearrange("p (h n) -> p h n", h=TH)
                                if l1:
                                    e_res.wait(eng, r.back(1))
                                    t3 = tmp[:, :].rearrange("p (h n) -> p h n", h=TH)
                                    for h in range(TH):
                                        ins = eng.tensor_tensor(t3[:, h], o3[:, h], gbc[r.par][:, 0:D], ALU.mult)
                                    e_tmp.by(ins)
                                    e_tmp.wait(eng, r)
                                    e_res.by(eng.tensor_tensor(x_at(r), t3, x3, ALU.add))
                                else:
                                    e_res.by(eng.tensor_tensor(x_at(r), o3, x3, ALU.add))
                            split(m, 1)
                            if f.exists(NB):
                                norm.normalize(eng, f)
                            split(m, 2)
                            if f.exists(NB):
                                norm.evac_lo(eng, f)
                            split(m, 3)
                        run_pipeline(eng, NB, 2, it)

                    @blk.gpsimd
                    def _(eng):
                        def it(i):
                            if i.exists(NB):
                                norm.root(eng, i)
                            m = i.back(1)
                            if m.exists(NB):
                                e_res.wait(eng, m.back(UNROLL))
                                if l1:
                                    eng.wait_ge(s_gin[m.par], (m.pair + 1) * 16)
                                for h in range(TH):
                                    ins = eng.tensor_tensor(xb[m.par][:, h * D:(h + 1) * D], x_at(m)[:, h],
                                                            gbc[m.par][:, D:2 * D] if l1 else bias2[:, :], ALU.add)
                                e_xb.by(ins)
                        run_pipeline(eng, NB, 2, it)

                    if l1:
                        @blk.sync
                        def _(eng):
                            gd = mod_dram[1].rearrange("(j u) n -> j u n", u=UNROLL)
                            od = out.rearrange("(j u) (h p) n -> j u p h n", u=UNROLL, p=P)

                            def it(i):
                                f, r = i, i.back(2)
                                if f.exists(NB):
                                    e_res.wait(eng, f.back(UNROLL))
                                    eng.dma_start(gbc[f.par][:, :], gd[f.pair, f.par].partition_broadcast(P))\
                                       .then_inc(s_gin[f.par], 16)
                                if r.exists(NB):
                                    e_res.wait(eng, r)
                                    eng.dma_start(od[r.pair, r.par], x_at(r)).then_inc(s_out[r.par], 16)
                            run_pipeline(eng, NB, 2, it)
                            for s in s_out:
                                eng.wait_ge(s, NB // UNROLL * 16)

        def phase_l1_attention():
            with ExitStack() as st:
                sb, ps, sem, event = allocator(st, "C_")
                sbank = banks[:2]
                stbank = banks[2:4]
                ybank, misc = banks[4], banks[5:8]
                bias_q, bias_k = sb("bias_q", [P, KT * NB]), sb("bias_k", [P, KT * NB])
                NT = NH // 2
                HALF = P // 2
                ROW_HI, ROW_LO = 3 * CH, 3 * CH + 1
                MAX_DMAS = 4
                sel = {n: sb("sel_" + n, [P, 4 * P], F32R) for n in ("q_hi", "q_lo", "k_hi", "k_lo")}
                keep_half = [sb(f"keep{e}", [P, 1]) for e in range(2)]
                one_rows = [sb(f"ones{e}", [P, 1]) for e in range(2)]
                vaug = [sb(f"vaug{u}", [P, TH * NH * 32]) for u in range(UNROLL)]
                held = hold_weights(sb, [("qkv", a["L1_cond_w_qkv"]), ("proj", a["L1_cond_w_proj"])])
                with ExitStack() as pre:
                    psb, _, psem, _ = allocator(pre, "Cp_")
                    ws = load_weights(psb, psem, held)
                    cv = psb("cv", [P, KT * NB])
                    brow, gate_row = psb("brow", [NB, D]), psb("gate_row", [NB, 2 * D])
                    seltmp = psb("seltmp", [P, 4 * P])
                    s_b, s_mm, s_cv, s_pj, s_g, s_z, s_m = (psem(n) for n in ("b", "mm", "cv", "pj", "g", "z", "m"))
                    with nc.Block() as blk:
                        @blk.sync
                        def _(eng):
                            emit_loads(eng, ws)
                            eng.dma_start(brow[:, :], a["L1_cond_b_proj"].partition_broadcast(NB)).then_inc(s_b, 16)
                            eng.wait_ge(s_g, 3)
                            eng.dma_start(mod_dram[0], gate_row[:, :]).then_inc(s_b, 16)
                            eng.wait_ge(s_b, 32)

                        @blk.scalar
                        def _(eng):
                            emit_hi(eng, ws)

                        @blk.gpsimd
                        def _(eng):
                            for u in range(UNROLL):
                                v4 = vaug[u][:, :].rearrange("p (k h c) -> p k h c", k=TH, c=32)
                                eng.memset(v4[:, :, :, CH:32], 1.0)
                            for e in range(2):
                                eng.memset(keep_half[e][:, :], 0.0).then_inc(s_m, 1)
                                eng.memset(one_rows[e][:, :], 1.0).then_inc(s_m, 1)
                            eng.wait_ge(s_m, 4)
                            for e in range(2):
                                eng.memset(keep_half[e][e * HALF:(e + 1) * HALF, :], 1.0).then_inc(s_m, 1)
                            eng.wait_ge(s_m, 6)
                            for e in range(2):
                                eng.affine_select(out=one_rows[e][:, :], in_=one_rows[e][:, :], compare_op=ALU.is_ge,
                                                  fill=0.0, base=-(e * HALF + ROW_HI), pattern=[[0, 1]],
                                                  channel_multiplier=1).then_inc(s_m, 1)
                            eng.wait_ge(s_m, 8)
                            for e in range(2):
                                eng.affine_select(out=one_rows[e][:, :], in_=one_rows[e][:, :], compare_op=ALU.is_ge,
                                                  fill=0.0, base=e * HALF + ROW_LO, pattern=[[0, 1]],
                                                  channel_multiplier=-1)

                        @blk.tensor
                        def _(eng):
                            for i, c0 in enumerate((D, 0, 2 * D)):
                                for t in range(KT):
                                    ins = shift_bias(eng, misc[0], (i * KT + t) * NB, ws["qkv"], c0 + t * P, shift1a)
                            ins.then_inc(s_mm, 1)
                            eng.wait_ge(s_cv, 1)
                            raw, _, _, t, N, _, s_in, _ = ws["proj"]
                            eng.wait_ge(s_in, 16)
                            for k in range(KT):
                                ins = eng.matmul(misc[1][0:NB, 0:D], cv[:, k * NB:(k + 1) * NB], raw[:, k * N:(k + 1) * N],
                                                 start=k == 0, stop=k == KT - 1)
                            ins.then_inc(s_pj, 1)

                        @blk.vector
                        def _(eng):
                            z = 0
                            for name in sel:
                                eng.wait_ge(s_z, z)
                                eng.memset(seltmp[:, :], 0.0).then_inc(s_z, 1)
                                z += 1
                                eng.wait_ge(s_z, z)
                                d5 = seltmp[:, :].rearrange("p (u e g c) -> p u e g c", u=4, e=2, c=CH)
                                i4 = ident[:, :].rearrange("p (u e c) -> p u e c", u=4, e=2)
                                for slot in {"q_hi": (0, 1), "q_lo": (2,), "k_hi": (0, 2), "k_lo": (1,)}[name]:
                                    eng.tensor_copy(d5[:, :, :, slot], i4).then_inc(s_z, 1)
                                    z += 1
                                eng.wait_ge(s_z, z)
                                eng.tensor_copy(sel[name][:, :], seltmp[:, :]).then_inc(s_z, 1)
                                z += 1
                            eng.wait_ge(s_mm, 1)
                            for i, dst in enumerate((bias_q, bias_k, cv)):
                                ins = eng.tensor_copy(dst[:, :], misc[0][:, i * KT * NB:(i + 1) * KT * NB])
                            ins.then_inc(s_cv, 1)
                            emit_lo(eng, ws)
                            eng.wait_ge(s_pj, 1)
                            eng.wait_ge(s_b, 16)
                            eng.tensor_copy(gate_row[:, 0:D], gates[:, 0:D]).then_inc(s_g, 1)
                            eng.tensor_tensor(brow[:, :], misc[1][0:NB, 0:D], brow[:, :], ALU.add).then_inc(s_g, 1)
                            eng.wait_ge(s_g, 2)
                            eng.tensor_tensor(gate_row[:, D:2 * D], gates[:, 0:D], brow[:, :], ALU.mult).then_inc(s_g, 1)

                qk = {n: sb(n, [P, KT * S], F32R) for n in ("q_hi", "q_lo", "k_hi", "k_lo")}
                qs = [sb(f"qs{u}", [P, NT * S], F32R) for u in range(UNROLL)]
                kx = [[sb(f"kx{u}{e}", [P, NT * S], F32R) for e in range(2)] for u in range(UNROLL)]
                NP = 8
                probs = [sb(f"probs{i}", [P, TH * S]) for i in range(NP)]
                negmax = sb("negmax", [P, TH * NH])
                mhl = [sb(f"mhl{w}", [NH // 2, 2 * S], F32R) for w in range(2)]
                ysb = [sb(f"ysb{w}", [P, 2 * S]) for w in range(2)]
                yrec = sb("yrec", [P, NH])
                ytok = sb("ytok", [P, TH * D])
                y_hi, y_lo = sb("y_hi", [P, KT * S], F32R), sb("y_lo", [P, KT * S], F32R)
                xb = sb("xb", [P, TH * D])
                gbc = [sb(f"gbc{u}", [P, 2 * D]) for u in range(UNROLL)]
                tmp = sb("tmp", [P, TH * D])
                e_q, e_k, e_v, e_y2, e_pr = (event(n) for n in ("q", "k", "v", "y2", "pr"))
                e_hiq, e_hik, e_loq, e_lok, e_vev = (event(n) for n in ("hiq", "hik", "loq", "lok", "vev"))
                e_sq, e_sk, e_sqev, e_skev0, e_skev1 = (event(n, 4) for n in ("sq", "sk", "sqev", "skev0", "skev1"))
                e_s, e_max, e_st, e_exp = (event(n, NH) for n in ("s", "max", "st", "exp"))
                e_mT, e_mhi, e_mlo = (event(n, 2) for n in ("mT", "mhi", "mlo"))
                s_mdma = [[sem(f"mdma{w}{u}") for u in range(UNROLL)] for w in range(2)]
                e_av = event("av", 4)
                e_ysb, e_y1, e_yrec, e_ytok = (event(n, 2) for n in ("ysb", "y1", "yrec", "ytok"))
                e_yhi, e_ylo = event("yhi"), event("ylo")
                e_xb, e_tmp, e_res = event("xb"), event("tmp"), event("res")
                s_gin = [sem(f"gin{u}") for u in range(UNROLL)]
                scl = 1.0 / CH

                ORDER = [(0, "M1", 2), (2, "v", 1), (3, "Y1b", 3), (4, "T", 0), (5, "Y2", 3), (6, "q", 0),
                         (7, "k", 0), (8, "PR", 3), (9, "M0", 1),
                         (10, "SQ0", 0), (10, "SK0", 0), (11, "Y1a", 2), (12, "SQ1", 0), (12, "SK1", 0),
                         (14, "SQ2", 0), (14, "SK2", 0), (15, "SQ3", 0), (15, "SK3", 0)]
                names = [n for _, n, _ in ORDER]
                skew = {n: k for _, n, k in ORDER}
                assert len(ORDER) % 3 == 0
                norm = Norm(sb, event, False, scale1a, misc[names.index("T") % 3], (e_v, 1))
                freed = {"M0": (e_mlo, 1), "M1": (e_mlo, 2), "v": (e_vev, 1), "Y1a": (e_ytok, 1), "Y1b": (e_ytok, 2),
                         "T": (norm.e_lo, 1), "Y2": (e_ylo, 1), "q": (e_loq, 1), "k": (e_lok, 1), "PR": (e_tmp, 1)}
                for u in range(4):
                    freed[f"SQ{u}"] = (e_sqev, u + 1)
                    freed[f"SK{u}"] = (e_skev1, u + 1)

                def mbank(name):
                    return misc[names.index(name) % 3]

                def bank_free(eng, name, i):
                    n = names.index(name)
                    while True:
                        n -= 3
                        if n < 0:
                            n += len(names)
                            i = i.back(1)
                        prev = i.back(skew[names[n]])
                        if i.before_first():
                            return
                        if prev.exists(NB):
                            ev, k = freed[names[n]]
                            ev.wait(eng, prev, k)
                            return

                with nc.Block() as blk:
                    @blk.tensor
                    def _(eng):
                        def scores(b, h):
                            t, e = divmod(h, 2)
                            if h % 4 == 0:
                                e_sqev.wait(eng, b, h // 4 + 1)
                                e_skev0.wait(eng, b, h // 4 + 1)
                                e_skev1.wait(eng, b, h // 4 + 1)
                            e_max.wait(eng, b, h - 1)
                            for qh in range(TH):
                                ins = eng.matmul(sbank[h % 2][:, qh * S:(qh + 1) * S],
                                                 qs[b.par][:, t * S + qh * P:t * S + (qh + 1) * P],
                                                 kx[b.par][e][:, t * S:(t + 1) * S], start=True, stop=True)
                            e_s.by(ins)

                        def scores_t(b, h):
                            t, e = divmod(h, 2)
                            if h % 8 == 0:
                                eng.wait_ge(s_mdma[h // 8][b.par], (b.pair + 1) * MAX_DMAS * 16)
                            e_exp.wait(eng, b, h - 1)
                            for kh in range(TH):
                                ins = eng.matmul(stbank[h % 2][:, kh * S:(kh + 1) * S],
                                                 kx[b.par][e][:, t * S + kh * P:t * S + (kh + 1) * P],
                                                 qs[b.par][:, t * S:(t + 1) * S], start=True, stop=True)
                            e_st.by(ins)

                        def weighted_v(b, g):
                            e_exp.wait(eng, b, 4 * g + 4)
                            if g == 0:
                                e_vev.wait(eng, b)
                                e_ysb.wait(eng, b.back(1), 2)
                            if g == 2:
                                e_ysb.wait(eng, b, 1)
                            for kh in range(TH):
                                for j in range(4):
                                    h = 4 * g + j
                                    v0 = (kh * NH + h) * 32
                                    ins = eng.matmul(ybank[32 * j:32 * j + 32, (g % 2) * S:(g % 2 + 1) * S],
                                                     vaug[b.par][:, v0:v0 + 32], probs[h % NP][:, kh * S:(kh + 1) * S],
                                                     start=kh == 0, stop=kh == TH - 1, skip_group_check=True)
                            e_av.by(ins)

                        def max_t(b, w):
                            e_max.wait(eng, b, 8 * w + 8)
                            for qh in range(TH):
                                ins = eng.transpose(mbank(f"M{w}")[0:NH // 2, qh * P:(qh + 1) * P],
                                                    negmax[:, qh * NH + 8 * w:qh * NH + 8 * w + 8], ident[:, :])
                            e_mT.by(ins)

                        def y_tok(b, w):
                            e_ysb.wait(eng, b, w + 1)
                            for qh in range(TH):
                                for g in range(2):
                                    c = (qh * 2 + g) * P
                                    ins = eng.transpose(mbank("Y1" + "ab"[w])[:, c:c + P],
                                                        ysb[w][:, g * S + qh * P:g * S + (qh + 1) * P], ident[:, :])
                            e_y1.by(ins)

                        def y_chan(b):
                            e_ytok.wait(eng, b)
                            for t in range(KT):
                                for h in range(TH):
                                    ins = eng.transpose(mbank("Y2")[:, t * S + h * P:t * S + (h + 1) * P],
                                                        ytok[:, h * D + t * P:h * D + (t + 1) * P], ident[:, :])
                            e_y2.by(ins)

                        def project(b):
                            e_ylo.wait(eng, b)
                            for h in range(TH):
                                ins = mm3(eng, mbank("PR")[:, h * D:(h + 1) * D], [
                                    ((y_hi[:, t * S + h * P:t * S + (h + 1) * P],
                                      y_lo[:, t * S + h * P:t * S + (h + 1) * P]),
                                     weight(ws["proj"], t, 0, D)) for t in range(KT)])
                            e_pr.by(ins)

                        def qk_cm(b, name, c0, done):
                            norm.e_lo.wait(eng, b)
                            for t in range(KT):
                                ins = mm3(eng, mbank(name)[:, t * S:(t + 1) * S],
                                          [(weight(ws["qkv"], k, c0 + t * P, P), norm.tokens(b, k)) for k in range(KT)])
                            done.by(ins)

                        def v_tok(b):
                            for h in range(TH):
                                ins = mm3(eng, mbank("v")[:, h * D:(h + 1) * D],
                                          [(norm.tokens(b, k, h), weight(ws["qkv"], k, 2 * D, D)) for k in range(KT)])
                            e_v.by(ins)

                        def stack(b, name, src, e_in, done, u):
                            if u == 0:
                                e_in.wait(eng, b)
                            for d in range(2):
                                t, uu = divmod(2 * u + d, 4)
                                for k, part in enumerate(("_hi", "_lo")):
                                    ins = eng.matmul(mbank(f"{name}{u}")[:, d * S:(d + 1) * S],
                                                     sel[src + part][:, uu * P:(uu + 1) * P],
                                                     qk[src + part][:, t * S:(t + 1) * S], start=k == 0, stop=k == 1)
                            done.by(ins)

                        def it(i):
                            f, m, b, r = i, i.back(1), i.back(2), i.back(3)
                            work = {"M1": lambda: max_t(b, 1), "M0": lambda: max_t(m, 0), "v": lambda: v_tok(m),
                                    "Y1a": lambda: y_tok(b, 0), "Y1b": lambda: y_tok(r, 1), "Y2": lambda: y_chan(r),
                                    "T": lambda: norm.transpose(eng, f), "q": lambda: qk_cm(f, "q", D, e_q),
                                    "k": lambda: qk_cm(f, "k", 0, e_k), "PR": lambda: project(r)}
                            for u in range(4):
                                work[f"SQ{u}"] = lambda u=u: stack(f, "SQ", "q", e_loq, e_sq, u)
                                work[f"SK{u}"] = lambda u=u: stack(f, "SK", "k", e_lok, e_sk, u)
                            for s in range(NH):
                                if m.exists(NB):
                                    scores(m, s)
                                if b.exists(NB):
                                    scores_t(b, s)
                                if s == 1 and r.exists(NB):
                                    weighted_v(r, 3)
                                if s in (5, 9, 13) and b.exists(NB):
                                    weighted_v(b, (s - 5) // 4)
                                for slot, name, k in ORDER:
                                    if slot == s and i.back(k).exists(NB):
                                        bank_free(eng, name, i)
                                        work[name]()
                        run_pipeline(eng, NB, 3, it)

                    @blk.scalar
                    def _(eng):
                        def exp(b, h):
                            e_st.wait(eng, b, h + 1)
                            e_av.wait(eng, b if h >= NP else b.back(1), (h - NP) // 4 + 1 if h >= NP else (h + NP) // 4 + 1)
                            e_exp.by(eng.activation(probs[h % NP][:, :], stbank[h % 2][:, :], ACT.Exp, scale=scl))

                        def hi_bias(b, name, dst, bias, e_in, e_out, e_reader):
                            e_in.wait(eng, b)
                            e_reader.wait(eng, b.back(1))
                            for t in range(KT):
                                c = slice(t * S, (t + 1) * S)
                                ins = eng.activation(dst[:, c], mbank(name)[:, c], ACT.Identity, bias=per_seq(bias, t, b))
                            e_out.by(ins)

                        def stack_q(b, u):
                            e_sq.wait(eng, b, u + 1)
                            e_st.wait(eng, b.back(2), 4 * u + 4)
                            e_sqev.by(eng.activation(qs[b.par][:, 2 * u * S:(2 * u + 2) * S], mbank(f"SQ{u}")[:, :], ACT.Copy))

                        def stack_k(b, u):
                            e_sk.wait(eng, b, u + 1)
                            e_skev0.by(eng.activation(kx[b.par][0][:, 2 * u * S:(2 * u + 2) * S], mbank(f"SK{u}")[:, :],
                                                      ACT.Identity, bias=one_rows[0][:, 0:1], scale=keep_half[0][:, 0:1]))

                        def max_hi(b, w):
                            e_mT.wait(eng, b, w + 1)
                            if True:
                                prev = b.back(1)
                                if not prev.before_first():
                                    eng.wait_ge(s_mdma[w][prev.par], (prev.pair + 1) * MAX_DMAS * 16)
                            e_mhi.by(eng.activation(mhl[w][:, 0:S], mbank(f"M{w}")[0:NH // 2, 0:S], ACT.Copy))

                        def y_out(b, w):
                            e_av.wait(eng, b, 2 * w + 2)
                            e_y1.wait(eng, b.back(1), w + 1)
                            e_ysb.by(eng.activation(ysb[w][:, :], ybank[:, :], ACT.Copy))

                        def it(i):
                            f, m, b, r = i, i.back(1), i.back(2), i.back(3)
                            for s in range(NH):
                                if b.exists(NB):
                                    exp(b, s)
                                if s == 0 and b.exists(NB):
                                    max_hi(b, 1)
                                if s == 2 and r.exists(NB):
                                    y_out(r, 1)
                                if s == 3 and m.exists(NB):
                                    e_v.wait(eng, m)
                                    e_av.wait(eng, m.back(2))
                                    v4 = vaug[m.par][:, :].rearrange("p (k h c) -> p k h c", k=TH, c=32)
                                    s4 = mbank("v")[:, :].rearrange("p (k h c) -> p k h c", k=TH, c=CH)
                                    for kh in range(TH):
                                        ins = eng.activation(v4[:, kh, :, 0:CH], s4[:, kh], ACT.Copy)
                                    e_vev.by(ins)
                                if s == 5 and f.exists(NB):
                                    norm.evac_hi(eng, f)
                                if s == 6 and r.exists(NB):
                                    e_y2.wait(eng, r)
                                    e_pr.wait(eng, r.back(1))
                                    e_yhi.by(eng.activation(y_hi[:, :], mbank("Y2")[:, :], ACT.Copy))
                                if s == 7 and f.exists(NB):
                                    hi_bias(f, "q", qk["q_hi"], bias_q, e_q, e_hiq, e_sq)
                                if s == 8 and f.exists(NB):
                                    hi_bias(f, "k", qk["k_hi"], bias_k, e_k, e_hik, e_sk)
                                if s == 10 and m.exists(NB):
                                    max_hi(m, 0)
                                if s == 10 and b.exists(NB):
                                    y_out(b, 0)
                                if s in (11, 13, 14, 15) and f.exists(NB):
                                    u = {11: 0, 13: 1, 14: 2, 15: 3}[s]
                                    stack_q(f, u)
                                    stack_k(f, u)
                        run_pipeline(eng, NB, 3, it)

                    @blk.vector
                    def _(eng):
                        n3 = negmax[:, :].rearrange("p (q h) -> p q h", q=TH)

                        def maximum(b, h):
                            e_s.wait(eng, b, h + 1)
                            if h % 8 == 0:
                                e_mT.wait(eng, b.back(1), h // 8 + 1)
                            e_max.by(eng.tensor_reduce(n3[:, :, h], sbank[h % 2][:, :].rearrange("p (q k) -> p q k", q=TH),
                                                       AX, ALU.max, negate=True))

                        def max_lo(b, w):
                            e_mhi.wait(eng, b, w + 1)
                            e_mlo.by(eng.tensor_tensor(mhl[w][:, S:2 * S], mbank(f"M{w}")[0:NH // 2, 0:S],
                                                       mhl[w][:, 0:S].bitcast(F32), ALU.subtract))

                        def lo_bias(b, name, hi, lo, bias, e_in, e_out):
                            e_in.wait(eng, b)
                            for t in range(KT):
                                c = slice(t * S, (t + 1) * S)
                                ins = eng.scalar_tensor_tensor(out=lo[:, c], in0=mbank(name)[:, c], scalar=per_seq(bias, t, b),
                                                               in1=hi[:, c].bitcast(F32), op0=ALU.add, op1=ALU.subtract)
                            e_out.by(ins)

                        def stack_k(b, u):
                            e_skev0.wait(eng, b, u + 1)
                            e_skev1.by(eng.tensor_scalar(kx[b.par][1][:, 2 * u * S:(2 * u + 2) * S], mbank(f"SK{u}")[:, :],
                                                         keep_half[1][:, 0:1], one_rows[1][:, 0:1], ALU.mult, ALU.add))

                        def y_norm(b, w):
                            e_y1.wait(eng, b, w + 1)
                            src = mbank("Y1" + "ab"[w])[:, :].rearrange("p (a c) -> p a c", c=32)
                            if w == 0:
                                e_ytok.wait(eng, b.back(1))
                            else:
                                e_ytok.wait(eng, b, 1)
                            e_yrec.by(eng.reciprocal(yrec[:, :], src[:, :, CH]))
                            e_yrec.wait(eng, b, w + 1)
                            if w == 0:
                                e_y2.wait(eng, b.back(1))
                            for q in range(TH):
                                r3 = yrec[:, q * 8:(q + 1) * 8].unsqueeze(2).broadcast_to([P, 8, CH])
                                o3 = ytok[:, q * D + w * P:q * D + (w + 1) * P].rearrange("p (a c) -> p a c", c=CH)
                                ins = eng.tensor_tensor(o3, src[:, q * 8:(q + 1) * 8, 0:CH], r3, ALU.mult)
                            e_ytok.by(ins)

                        def it(i):
                            f, m, b, r = i, i.back(1), i.back(2), i.back(3)
                            for s in range(NH):
                                if m.exists(NB):
                                    maximum(m, s)
                                if s == 0 and b.exists(NB):
                                    max_lo(b, 1)
                                if s == 1 and f.exists(NB):
                                    norm.stats(eng, f)
                                if s == 3 and r.exists(NB):
                                    y_norm(r, 1)
                                if s == 3 and f.exists(NB):
                                    norm.normalize(eng, f)
                                if s == 5 and f.exists(NB):
                                    norm.evac_lo(eng, f)
                                if s == 6 and r.exists(NB):
                                    e_yhi.wait(eng, r)
                                    e_ylo.by(eng.tensor_tensor(y_lo[:, :], mbank("Y2")[:, :], y_hi[:, :].bitcast(F32),
                                                               ALU.subtract))
                                if s == 7 and f.exists(NB):
                                    lo_bias(f, "q", qk["q_hi"], qk["q_lo"], bias_q, e_hiq, e_loq)
                                if s == 8 and f.exists(NB):
                                    lo_bias(f, "k", qk["k_hi"], qk["k_lo"], bias_k, e_hik, e_lok)
                                if s == 9 and r.exists(NB):
                                    e_pr.wait(eng, r)
                                    e_res.wait(eng, r.back(1))
                                    e_xb.wait(eng, r)
                                    p3 = mbank("PR")[:, :].rearrange("p (h n) -> p h n", h=TH)
                                    t3 = tmp[:, :].rearrange("p (h n) -> p h n", h=TH)
                                    for h in range(TH):
                                        ins = eng.tensor_tensor(t3[:, h], p3[:, h], gbc[r.par][:, 0:D], ALU.mult)
                                    e_tmp.by(ins)
                                    e_tmp.wait(eng, r)
                                    e_res.by(eng.tensor_tensor(x_at(r), t3, xb[:, :].rearrange("p (h n) -> p h n", h=TH),
                                                               ALU.add))
                                if s == 10 and m.exists(NB):
                                    max_lo(m, 0)
                                if s == 12 and b.exists(NB):
                                    y_norm(b, 0)
                                if s in (11, 13, 14, 15) and f.exists(NB):
                                    stack_k(f, {11: 0, 13: 1, 14: 2, 15: 3}[s])
                        run_pipeline(eng, NB, 3, it)

                    @blk.gpsimd
                    def _(eng):
                        def it(i):
                            if i.exists(NB):
                                norm.root(eng, i)
                            r = i.back(3)
                            if r.exists(NB):
                                e_res.wait(eng, r.back(1))
                                eng.wait_ge(s_gin[r.par], (r.pair + 1) * 16)
                                for h in range(TH):
                                    ins = eng.tensor_tensor(xb[:, h * D:(h + 1) * D], x_at(r)[:, h], gbc[r.par][:, D:2 * D],
                                                            ALU.add)
                                e_xb.by(ins)
                        run_pipeline(eng, NB, 3, it)

                    @blk.sync
                    def _(eng):
                        gd = mod_dram[0].rearrange("(j u) n -> j u n", u=UNROLL)

                        def place_max(b, w):
                            e_mlo.wait(eng, b, w + 1)
                            for e in range(2):
                                for c, r0 in enumerate((ROW_HI, ROW_LO)):
                                    row = e * HALF + r0
                                    dst = qs[b.par][row:row + 1, 4 * w * S:(4 * w + 4) * S]
                                    eng.dma_start(dst.bitcast(F32).rearrange("p (t n) -> p t n", t=4),
                                                  mhl[w][e:NH // 2:2, c * S:(c + 1) * S].bitcast(F32))\
                                       .then_inc(s_mdma[w][b.par], 16)

                        def it(i):
                            m, b, r = i.back(1), i.back(2), i.back(3)
                            if b.exists(NB):
                                place_max(b, 1)
                            if b.exists(NB):
                                e_res.wait(eng, b.back(UNROLL))
                                eng.dma_start(gbc[b.par][:, :], gd[b.pair, b.par].partition_broadcast(P))\
                                   .then_inc(s_gin[b.par], 16)
                            if m.exists(NB):
                                place_max(m, 0)
                        run_pipeline(eng, NB, 3, it)

        phase_l0_attention()
        phase_mlp(0)
        phase_l1_attention()
        phase_mlp(1)


def kernel(**inputs):
    import numpy as np
    import concourse.bacc as bacc
    from concourse.bass_utils import run_bass_kernel_spmd

    nc = bacc.Bacc("TRN2", target_bir_lowering=False, num_devices=1)
    arrays, aps = {}, {}
    for name, value in inputs.items():
        v = np.ascontiguousarray(value)
        arrays[f"in_{name}"] = v
        aps[name] = nc.dram_tensor(f"in_{name}", v.shape, mybir.dt.from_np(v.dtype), kind="ExternalInput").ap()
    out = nc.dram_tensor("out", aps["x"].shape, F32, kind="ExternalOutput").ap()
    nb, _, d = aps["x"].shape
    mod_dram = nc.dram_tensor("mod_rows", [3, nb, 2 * d], F32, kind="Internal").ap()
    build(nc, aps, out, mod_dram)
    r = run_bass_kernel_spmd(nc, [arrays], core_ids=[0])
    return r.results[0]["out"]
```

```python
from contextlib import ExitStack

import concourse.bass as bass
from concourse import mybir
from concourse.alu_op_type import AluOpType as ALU

F32 = mybir.dt.float32
F32R = mybir.dt.float32r
ACT = mybir.ActivationFunctionType
AX = mybir.AxisListType.X

P = 128
EPS = 1e-6
UNROLL = 2
PEEL = 4


class Seq:

    def __init__(self, reg, off):
        self.reg, self.off = reg, off

    def back(self, n):
        return Seq(self.reg, self.off - n)

    @property
    def par(self):
        return self.off % UNROLL

    @property
    def num(self):
        return self.off if self.reg is None else self.reg * UNROLL + self.off

    @property
    def pair(self):
        return self.off // UNROLL if self.reg is None else self.reg + self.off // UNROLL

    def before_first(self):
        return self.reg is None and self.off < 0

    def exists(self, n):
        return self.reg is not None or 0 <= self.off < n


class Event:

    def __init__(self, sem, per, base=0):
        self.sem, self.per, self.base = sem, per, base

    def by(self, instruction):
        instruction.then_inc(self.sem, 1)

    def wait(self, eng, seq, k=None):
        k = self.per if k is None else k
        if seq.reg is not None or seq.off * self.per + k > 0:
            eng.wait_ge(self.sem, seq.num * self.per + self.base + k)


def run_pipeline(eng, n_seq, max_skew, iteration):
    for i in range(PEEL):
        iteration(Seq(None, i))
    with eng.Fori(PEEL // UNROLL, n_seq // UNROLL) as j:
        for u in range(UNROLL):
            iteration(Seq(j, u))
    for i in range(n_seq, n_seq + max_skew):
        iteration(Seq(None, i))


def build(nc, a, out, mod_dram):
    NB, S, D = a["x"].shape
    TH, KT = S // P, D // P
    HID = a["L0_cond_mlp_w1"].shape[1]
    HT = HID // P
    NH, CH = 16, D // 16
    assert TH == 2 and KT == 2 and HT == 8 and NB % UNROLL == 0

    root, semaphores, events = ExitStack(), ExitStack(), {}

    def allocator(stack, prefix):
        def sb(name, shape, dt=F32):
            return stack.enter_context(nc.sbuf_tensor(prefix + name, shape, dt))

        def ps(name, shape, dt=F32):
            return stack.enter_context(nc.psum_tensor(prefix + name, shape, dt))

        def sem(name):
            return semaphores.enter_context(nc.semaphore(prefix + name))

        def event(name, per=1):
            if name in events:
                old = events[name]
                assert old.per == per
                events[name] = Event(old.sem, per, old.base + NB * per)
            else:
                events[name] = Event(semaphores.enter_context(nc.semaphore("e_" + name)), per)
            return events[name]
        return sb, ps, sem, event

    with semaphores, root:
        sb, ps, sem, event = allocator(root, "")
        xres = sb("xres", [P, NB * TH * D])
        xv = xres[:, :].rearrange("p (j u h n) -> p j u h n", u=UNROLL, h=TH, n=D)
        ident = sb("ident", [P, P])
        banks = [ps(f"bank{i}", [P, 512]) for i in range(8)]
        neghalf = sb("neghalf", [P, TH])
        scale0a, shift0a = sb("scale0a", [P, KT * NB]), sb("shift0a", [P, KT * NB])
        scale0m, shift0m = sb("scale0m", [P, KT * NB]), sb("shift0m", [P, KT * NB])
        scale1a, shift1a = sb("scale1a", [P, KT * NB]), sb("shift1a", [P, KT * NB])
        scale1m, shift1m = sb("scale1m", [P, KT * NB]), sb("shift1m", [P, KT * NB])
        gates = sb("gates", [NB, 2 * D])
        STAGE = KT * HID
        stage = [sb("stage0", [P, STAGE])]

        def staged_weights(phase, specs):
            found, at = {}, 0
            for key, v in specs:
                found[key] = divmod(at, STAGE), v, sem(f"{phase}_{key}_in")
                at += v.shape[0] // P * v.shape[1]
            return found

        def raw(entry):
            (half, col), v, _ = entry
            return stage[half][:, col:col + v.shape[0] // P * v.shape[1]]

        def preload(eng, entries):
            for entry in entries:
                _, view, s_in = entry
                eng.dma_start(raw(entry).rearrange("p (t n) -> p t n", t=view.shape[0] // P),
                              view.rearrange("(t p) n -> p t n", p=P)).then_inc(s_in, 16)

        staged = {
            "B": staged_weights("B", [("w1", a["L0_cond_mlp_w1"]), ("w2", a["L0_cond_mlp_w2"])]),
            "C": staged_weights("C", [(n, a["L1_cond_w_qkv"][:, c:c + D]) for n, c in (("k", 0), ("q", D), ("v", 2 * D))] +
                                [("proj", a["L1_cond_w_proj"])]),
            "D": staged_weights("D", [("w1", a["L1_cond_w_mlp1"]), ("w2", a["L1_cond_w_mlp2"])])}

        sel = {n: sb("sel_" + n, [P, 4 * P], F32R) for n in ("hi", "lo")}

        def x_at(seq):
            return xv[:, seq.pair, seq.par]

        def per_seq(t, tile, seq):
            v = t[:, :].rearrange("p (t j u) -> p t j u", j=NB // UNROLL, u=UNROLL)
            return v[:, tile, seq.pair, seq.par:seq.par + 1]

        def mm3(eng, out_ap, pairs, start=True, stop=True, skip=False):
            last = None
            n = len(pairs)
            for i, ((a_hi, a_lo), (b_hi, b_lo)) in enumerate(pairs):
                for k, (l, r) in enumerate(((a_lo, b_hi), (a_hi, b_lo), (a_hi, b_hi))):
                    last = eng.matmul(out_ap, l, r, start=start and i == 0 and k == 0,
                                      stop=stop and i == n - 1 and k == 2, skip_group_check=skip)
            return last

        SLOTS, MAX_SKEW = 16, 3

        def schedule(early, *tables):
            tasks = [(t + early, n) for table in tables for n, t in table.items()]
            assert all(0 <= t < SLOTS * (MAX_SKEW + 1) for t, _ in tasks)
            return [(int(t // SLOTS), n) for t, n in sorted(tasks, key=lambda task: task[0] % SLOTS)]

        def run_tasks(eng, order, tasks, before=lambda name, b: None, once=()):
            def it(i):
                for k, name in order:
                    if i.back(k).exists(NB) and (name not in once or i.reg is None and i.off == k):
                        before(name, i.back(k))
                        tasks[name](i.back(k))
            run_pipeline(eng, NB, MAX_SKEW, it)

        class Norm:

            def __init__(self, sb, event, rms, scale, bank, reader):
                self.rms, self.scale, self.bank, self.reader = rms, scale, bank, reader
                self.stat = sb("stat", [P, TH * 6])
                self.mv = sb("mv", [P, TH * 2])
                self.var = sb("var", [P, TH])
                self.msq = sb("msq", [P, TH])
                self.rstd = sb("rstd", [P, TH])
                self.xhat = sb("xhat", [P, TH * D])
                self.hi = [sb(f"h_hi{u}", [P, KT * S], F32R) for u in range(UNROLL)]
                self.lo = [sb(f"h_lo{u}", [P, KT * S], F32R) for u in range(UNROLL)]
                self.e_mv = event("mv")
                self.e_msq = event("msq") if rms else None
                self.e_var = event("var")
                self.e_rstd = event("rstd")
                self.e_xhat = event("xhat")
                self.e_T = event("T")
                self.e_hi = event("hhi")
                self.e_lo = event("hlo")

            def stats(self, eng, b, x_in=None):
                if x_in is not None:
                    s, dmas = x_in[0 if b.reg is None and b.off < PEEL else 1]
                    eng.wait_ge(s, 16 * dmas)
                mv = self.mv[:, :].rearrange("p (h c) -> p h c", c=2)
                self.e_rstd.wait(eng, b.back(1))
                self.e_xhat.wait(eng, b.back(1))
                for h in range(TH):
                    eng.bn_stats(self.stat[:, 6 * h:6 * h + 6], x_at(b)[:, h])
                eng.drain()
                for h in range(TH):
                    ins = eng.bn_aggr(self.mv[:, 2 * h:2 * h + 2], self.stat[:, 6 * h:6 * h + 6])
                self.e_mv.by(ins)
                self.e_mv.wait(eng, b)
                if self.rms:
                    self.e_msq.by(eng.tensor_tensor(self.msq[:, :], mv[:, :, 0], mv[:, :, 0], ALU.mult))
                    self.e_msq.wait(eng, b)
                    ins = eng.scalar_tensor_tensor(out=self.var[:, :], in0=self.msq[:, :], scalar=EPS,
                                                   in1=mv[:, :, 1], op0=ALU.add, op1=ALU.add)
                else:
                    ins = eng.tensor_scalar(self.var[:, :], mv[:, :, 1], EPS, None, ALU.add)
                self.e_var.by(ins)

            def root(self, eng, b):
                self.e_var.wait(eng, b)
                self.e_xhat.wait(eng, b.back(1))
                self.e_rstd.by(eng.tensor_tensor(self.rstd[:, :], self.var[:, :], neghalf[:, :], ALU.pow))

            def normalize(self, eng, b):
                self.e_rstd.wait(eng, b)
                self.e_T.wait(eng, b.back(1))
                for h in range(TH):
                    r = self.rstd[:, h:h + 1]
                    o = self.xhat[:, h * D:(h + 1) * D]
                    if eng is nc.scalar:
                        ins = eng.activation(o, x_at(b)[:, h], ACT.Copy, scale=r)
                    elif self.rms:
                        ins = eng.tensor_scalar(o, x_at(b)[:, h], r, None, ALU.mult)
                    else:
                        ins = eng.tensor_scalar(o, x_at(b)[:, h], self.mv[:, 2 * h:2 * h + 1], r,
                                                ALU.subtract, ALU.mult)
                self.e_xhat.by(ins)

            def transpose(self, eng, b):
                self.e_xhat.wait(eng, b)
                for t in range(KT):
                    for h in range(TH):
                        ins = eng.transpose(self.bank[:, t * S + h * P:t * S + (h + 1) * P],
                                            self.xhat[:, h * D + t * P:h * D + (t + 1) * P], ident[:, :])
                self.e_T.by(ins)

            def evac_hi(self, eng, b):
                self.e_T.wait(eng, b)
                ev, k = self.reader
                ev.wait(eng, b.back(UNROLL), k)
                for t in range(KT):
                    ins = eng.activation(self.hi[b.par][:, t * S:(t + 1) * S], self.bank[:, t * S:(t + 1) * S],
                                         ACT.Copy, scale=per_seq(self.scale, t, b))
                self.e_hi.by(ins)

            def evac_lo(self, eng, b):
                self.e_hi.wait(eng, b)
                for t in range(KT):
                    c = slice(t * S, (t + 1) * S)
                    ins = eng.scalar_tensor_tensor(out=self.lo[b.par][:, c], in0=self.bank[:, c],
                                                   scalar=per_seq(self.scale, t, b),
                                                   in1=self.hi[b.par][:, c].bitcast(F32),
                                                   op0=ALU.mult, op1=ALU.subtract)
                self.e_lo.by(ins)

            def tokens(self, b, t, h=None):
                c = slice(t * S, (t + 1) * S) if h is None else slice(t * S + h * P, t * S + (h + 1) * P)
                return self.hi[b.par][:, c], self.lo[b.par][:, c]

        def hold_weights(sb, specs):
            return {key: (sb("wt_" + key + "_hi", [P, v.shape[0] // P * v.shape[1]], F32R),
                          sb("wt_" + key + "_lo", [P, v.shape[0] // P * v.shape[1]], F32R), v) for key, v in specs}

        def load_weights(sem, held, raws):
            return {key: (raws[key][0], hi, lo, v.shape[0] // P, v.shape[1], v, raws[key][1], sem(key + "_sp"))
                    for key, (hi, lo, v) in held.items()}

        def emit_hi(eng, ws):
            for raw, hi, lo, t, N, view, s_in, s_sp in ws.values():
                eng.wait_ge(s_in, 16)
                eng.activation(hi[:, :], raw[:, :], ACT.Copy).then_inc(s_sp, 1)

        def emit_lo(eng, ws):
            for raw, hi, lo, t, N, view, s_in, s_sp in ws.values():
                eng.wait_ge(s_sp, 1)
                eng.tensor_tensor(lo[:, :], raw[:, :], hi[:, :].bitcast(F32), ALU.subtract)

        def shift_bias(eng, psum, col, w, c0, shift):
            raw, _, _, t, N, _, s_in, _ = w
            eng.wait_ge(s_in, 16)
            for k in range(KT):
                ins = eng.matmul(psum[:, col:col + NB], raw[:, k * N + c0:k * N + c0 + P],
                                 shift[:, k * NB:(k + 1) * NB], start=k == 0, stop=k == KT - 1)
            return ins

        def weight(w, k, c0, n):
            _, hi, lo, t, N, *_ = w
            return hi[:, k * N + c0:k * N + c0 + n], lo[:, k * N + c0:k * N + c0 + n]

        def phase_l0_attention():
            with ExitStack() as st:
                sb, ps, sem, event = allocator(st, "A_")
                bT, bQ, _, bV, bS, bPT, bR, pmod = banks
                scl = float(D) ** -0.5
                biasq = sb("biasq", [P, KT * NB])
                m_hi, m_lo = sb("m_hi", [P, KT * D], F32R), sb("m_lo", [P, KT * D], F32R)
                vp_hi, vp_lo = sb("vp_hi", [P, KT * D], F32R), sb("vp_lo", [P, KT * D], F32R)
                condT, actT = sb("condT", [P, KT * NB]), sb("actT", [P, KT * NB])
                w_film2, w_ada = sb("w_film2", [P, KT * 2 * D]), sb("w_ada", [P, KT * 6 * D])
                b_film2, b_ada, n2 = sb("b_film2", [P, 4]), sb("b_ada", [P, 12]), sb("n2", [P, KT])
                b_gate = sb("b_gate", [NB, 2 * D])
                s_f2, s_ada, s_late, s_mod, s_gate, s_fix2 = (sem(n) for n in ("f2", "ada", "late", "mod", "gate", "fix2"))
                X_REST = 4
                x_in = ((sem("x_first"), 1), (sem("x_rest"), X_REST))

                def load_x(eng, first, n, s):
                    xd = a["x"].rearrange("b (h p) n -> p (b h) n", p=P)
                    xs = xres[:, :].rearrange("p (t n) -> p t n", n=D)
                    c = slice(first * TH, (first + n) * TH)
                    eng.dma_start(xs[:, c], xd[:, c]).then_inc(s, 16)

                def modulation(eng, w, width, cols, rhs, bank, slot):
                    for c in cols:
                        for t in range(KT):
                            m = eng.matmul(bank[:, slot * NB:(slot + 1) * NB],
                                           w[:, t * width + c * P:t * width + (c + 1) * P],
                                           rhs[:, t * NB:(t + 1) * NB], start=t == 0, stop=t == KT - 1)
                        slot += 1
                    return m

                def add_bias(eng, bank, slot, dst, b, lo, norm_w):
                    for t in range(KT):
                        src, o = bank[:, (slot + t) * NB:(slot + t + 1) * NB], dst[:, t * NB:(t + 1) * NB]
                        if norm_w is None:
                            ins = eng.tensor_scalar(o, src, b[:, lo + t:lo + t + 1], None, ALU.add)
                        else:
                            ins = eng.tensor_scalar(o, src, b[:, lo + t:lo + t + 1], norm_w[:, t:t + 1], ALU.add, ALU.mult)
                    return ins

                with ExitStack() as pre:
                    psb, _, psem, _ = allocator(pre, "Ap_")
                    w_q, w_k, w_v, w_p = (psb(n, [P, KT * D]) for n in ("w_q", "w_k", "w_v", "w_p"))
                    w_qT, w_kT, w_vT = (psb(n, [P, KT * D]) for n in ("w_qT", "w_kT", "w_vT"))
                    w_m, w_vp = psb("w_m", [P, KT * D]), psb("w_vp", [P, KT * D])
                    biasj = psb("biasj", [P, KT * NB])
                    cond, esig = psb("cond", [NB, D]), psb("esig", [P, KT * NB])
                    w_film1, b_film1, n1 = psb("w_film1", [P, KT * 2 * D]), psb("b_film1", [P, 4]), psb("n1", [P, KT])
                    biaso = psb("biaso", [P, KT * NB])
                    orow = psb("orow", [NB, D])
                    bcol = [psb(n, [P, KT]) for n in ("bq", "bv")]
                    s_cond, s_f1, s_b1, s_id, s_T, s_cT, s_e, s_fix = (
                        psem(n) for n in ("cond", "f1", "b1", "id", "T", "cT", "e", "fix"))
                    s_f1m, s_s0, s_vph = psem("f1m"), psem("s0"), psem("vph")
                    s_b, s_mm, s_vp, s_vT, s_vpm, s_cp, s_row = (psem(n) for n in ("b", "mm", "vp", "vT", "vpm", "cp", "row"))
                    s_kT = psem("kT")
                    s_qk, s_m, s_bq, s_z = (psem(n) for n in ("qk", "m", "bq", "z"))
                    seltmp = psb("seltmp", [P, 4 * P])
                    psh, pT, pvp, prow, pf1, pc, pqT, pkT = banks
                    pm, pbq = pf1, pc
                    with nc.Block() as blk:
                        @blk.sync
                        def _(eng):
                            def load(w, v, s):
                                eng.dma_start(w[:, :].rearrange("p (t n) -> p t n", t=KT),
                                              v.rearrange("(t p) n -> p t n", p=P)).then_inc(s, 16)
                            eng.dma_start(cond[:, :], a["cond_1024"]).then_inc(s_cond, 16)
                            load(w_film1, a["L0_cond_film1_w"], s_f1)
                            load(w_v, a["L0_cond_v_w"], s_vp)
                            load(w_p, a["L0_cond_proj_w"], s_vp)
                            load(w_q, a["L0_cond_q_w"], s_qk)
                            load(w_k, a["L0_cond_k_w"], s_qk)
                            load_x(eng, 0, PEEL, x_in[0][0])
                            load(w_film2, a["L0_cond_film2_w"], s_f2)
                            eng.wait_ge(s_row, 2)
                            eng.dma_start(mod_dram[2, :, 0:D], orow[:, :]).then_inc(s_row, 16)
                            eng.wait_ge(s_row, 2 + 16)

                        @blk.gpsimd
                        def _(eng):
                            eng.memset(neghalf[:, :], -0.5)
                            eng.memset(ident[:, :], 0.0).then_inc(s_id, 1)
                            eng.wait_ge(s_id, 1)
                            eng.affine_select(out=ident[:, :], in_=ident[:, :], compare_op=ALU.not_equal, fill=1.0,
                                              base=0, pattern=[[-1, P]], channel_multiplier=1).then_inc(s_id, 1)
                            with nc.allow_non_contiguous_dma(reason="bias vectors, one element per partition"):
                                for t, v, s in [(b_film1, a["L0_cond_film1_b"], s_b1), (n1, a["L0_cond_norm1_w"], s_b1)] + [
                                        (t, a[f"L0_cond_{k}_b"], s_b) for t, k in zip(bcol, "qv")]:
                                    eng.dma_start(t[:, :], v.rearrange("(t p) -> p t", p=P)).then_inc(s, 16)
                            eng.dma_start(orow[:, :], a["L0_cond_proj_b"].partition_broadcast(NB)).then_inc(s_b, 16)

                        @blk.scalar
                        def _(eng):
                            eng.wait_ge(s_cT, 1)
                            eng.activation(esig[:, :], condT[:, :], ACT.Exp, scale=-1.0).then_inc(s_e, 1)
                            with nc.allow_non_contiguous_dma(reason="bias vectors, one element per partition"):
                                for t, v in ((b_film2, a["L0_cond_film2_b"]), (b_ada, a["L1_cond_b_ada"]),
                                             (n2, a["L0_cond_norm2_w"])):
                                    eng.dma_start(t[:, :], v.rearrange("(t p) -> p t", p=P)).then_inc(s_late, 16)
                            for g, lo in enumerate((2 * D, 5 * D)):
                                eng.dma_start(b_gate[:, g * D:(g + 1) * D],
                                              a["L1_cond_b_ada"][lo:lo + D].partition_broadcast(NB)).then_inc(s_late, 16)
                            eng.wait_ge(s_cp, 2)
                            eng.activation(vp_hi[:, :], w_vp[:, :], ACT.Copy).then_inc(s_vph, 1)
                            eng.wait_ge(s_m, 2)
                            eng.activation(m_hi[:, :], w_m[:, :], ACT.Copy).then_inc(s_m, 1)

                        @blk.tensor
                        def _(eng):
                            eng.wait_ge(s_cond, 16)
                            eng.wait_ge(s_id, 2)
                            for t in range(KT):
                                m = eng.transpose(pc[:, t * NB:(t + 1) * NB], cond[:, t * P:(t + 1) * P], ident[0:NB, 0:NB])
                            m.then_inc(s_T, 1)
                            eng.wait_ge(s_f1, 16)
                            eng.wait_ge(s_cT, 1)
                            modulation(eng, w_film1, 2 * D, range(4), condT, pf1, 0).then_inc(s_f1m, 1)

                            def transpose_w(w, bank):
                                for c in range(KT):
                                    for r in range(KT):
                                        ins = eng.transpose(bank[:, c * D + r * P:c * D + (r + 1) * P],
                                                            w[:, r * D + c * P:r * D + (c + 1) * P], ident[:, :])
                                return ins

                            def product(bank, aT, b):
                                for r in range(KT):
                                    for c in range(KT):
                                        ins = eng.matmul(bank[:, r * D:(r + 1) * D], aT[:, c * D + r * P:c * D + (r + 1) * P],
                                                         b[:, c * D:(c + 1) * D], start=c == 0, stop=c == KT - 1)
                                return ins

                            eng.wait_ge(s_vp, 32)
                            transpose_w(w_v, pT).then_inc(s_vT, 1)
                            eng.wait_ge(s_qk, 32)
                            transpose_w(w_q, pqT)
                            transpose_w(w_k, pkT).then_inc(s_vT, 1)
                            eng.wait_ge(s_s0, 1)
                            modulation(eng, w_q, D, range(KT), shift0a, psh, 0)
                            modulation(eng, w_v, D, range(KT), shift0a, psh, KT).then_inc(s_mm, 1)
                            eng.wait_ge(s_cp, 1)
                            product(pvp, w_vT, w_p).then_inc(s_vpm, 1)
                            eng.wait_ge(s_kT, 1)
                            product(pm, w_qT, w_kT).then_inc(s_m, 1)
                            eng.wait_ge(s_bq, 1)
                            modulation(eng, w_kT, D, range(KT), biasj, pbq, 0).then_inc(s_bq, 1)
                            for k in range(KT):
                                ins = eng.matmul(prow[0:NB, 0:D], biaso[:, k * NB:(k + 1) * NB], w_p[:, k * D:(k + 1) * D],
                                                 start=k == 0, stop=k == KT - 1)
                            ins.then_inc(s_row, 1)

                        @blk.vector
                        def _(eng):
                            eng.wait_ge(s_T, 1)
                            eng.tensor_copy(condT[:, :], pc[:, 0:KT * NB]).then_inc(s_cT, 1)
                            eng.wait_ge(s_e, 1)
                            eng.tensor_scalar(esig[:, :], esig[:, :], 1.0, None, ALU.add).then_inc(s_fix, 1)
                            eng.wait_ge(s_fix, 1)
                            eng.reciprocal(actT[:, :], esig[:, :]).then_inc(s_fix, 1)
                            eng.wait_ge(s_fix, 2)
                            eng.tensor_tensor(actT[:, :], actT[:, :], condT[:, :], ALU.mult)
                            eng.wait_ge(s_id, 2)
                            z = 0
                            for name in sel:
                                eng.wait_ge(s_z, z)
                                eng.memset(seltmp[:, :], 0.0).then_inc(s_z, 1)
                                z += 1
                                eng.wait_ge(s_z, z)
                                d5 = seltmp[:, :].rearrange("p (u e g c) -> p u e g c", u=4, e=2, c=CH)
                                i4 = ident[:, :].rearrange("p (u e c) -> p u e c", u=4, e=2)
                                for slot in {"hi": (0, 1), "lo": (2,)}[name]:
                                    eng.tensor_copy(d5[:, :, :, slot], i4).then_inc(s_z, 1)
                                    z += 1
                                eng.wait_ge(s_z, z)
                                eng.tensor_copy(sel[name][:, :], seltmp[:, :]).then_inc(s_z, 1)
                                z += 1
                            eng.wait_ge(s_b1, 32)
                            eng.tensor_scalar(b_film1[:, 0:2], b_film1[:, 0:2], 1.0, None, ALU.add).then_inc(s_fix, 1)
                            eng.wait_ge(s_fix, 3)
                            eng.wait_ge(s_f1m, 1)
                            add_bias(eng, pf1, 0, scale0a, b_film1, 0, n1)
                            add_bias(eng, pf1, 2, shift0a, b_film1, 2, None).then_inc(s_s0, 1)
                            eng.wait_ge(s_vT, 1)
                            eng.tensor_copy(w_vT[:, :], pT[:, :]).then_inc(s_cp, 1)
                            eng.wait_ge(s_vT, 2)
                            eng.tensor_copy(w_qT[:, :], pqT[:, :])
                            eng.tensor_copy(w_kT[:, :], pkT[:, :]).then_inc(s_kT, 1)
                            eng.wait_ge(s_b, 16 * 3)
                            eng.wait_ge(s_mm, 1)
                            for i, dst in enumerate((biasj, biaso)):
                                for t in range(KT):
                                    c = (i * KT + t) * NB
                                    ins = eng.tensor_scalar(dst[:, t * NB:(t + 1) * NB], psh[:, c:c + NB],
                                                            bcol[i][:, t:t + 1], None, ALU.add)
                            ins.then_inc(s_bq, 1)
                            eng.wait_ge(s_vpm, 1)
                            eng.tensor_copy(w_vp[:, :], pvp[:, :]).then_inc(s_cp, 1)
                            eng.wait_ge(s_m, 1)
                            eng.tensor_scalar(w_m[:, :], pm[:, :], scl, None, ALU.mult).then_inc(s_m, 1)
                            eng.wait_ge(s_bq, 2)
                            eng.tensor_scalar(biasq[:, :], pbq[:, 0:KT * NB], scl, None, ALU.mult)
                            eng.wait_ge(s_row, 1)
                            eng.tensor_tensor(orow[:, :], prow[0:NB, 0:D], orow[:, :], ALU.add).then_inc(s_row, 1)
                            eng.wait_ge(s_vph, 1)
                            eng.tensor_tensor(vp_lo[:, :], w_vp[:, :], vp_hi[:, :].bitcast(F32), ALU.subtract)
                            eng.wait_ge(s_m, 3)
                            eng.tensor_tensor(m_lo[:, :], w_m[:, :], m_hi[:, :].bitcast(F32), ALU.subtract)

                def film2_products(eng):
                    eng.wait_ge(s_f2, 16)
                    modulation(eng, w_film2, 2 * D, range(4), condT, pmod, 0)

                def ada_products(eng, cols, slot):
                    eng.wait_ge(s_ada, 16)
                    modulation(eng, w_ada, 6 * D, cols, actT, pmod, slot).then_inc(s_mod, 1)

                def gate_products(eng):
                    eng.wait_ge(s_fix2, 4)
                    for g, lo in enumerate((2 * D, 5 * D)):
                        for t in range(KT):
                            m = eng.matmul(pmod[0:NB, g * D:(g + 1) * D], actT[:, t * NB:(t + 1) * NB],
                                           w_ada[:, t * 6 * D + lo:t * 6 * D + lo + D], start=t == 0, stop=t == KT - 1)
                    m.then_inc(s_gate, 1)

                LATE_PE = {"film2": 2, "ada0": 22.5, "ada1": 40, "gates": 59}
                LATE_DVE = {"modulation": 56}
                LATE_SP = {"ada": 0, "late loads": 48}

                def late_modulation(eng):
                    eng.wait_ge(s_late, 16 * 5)
                    for b, lo in ((b_film2, 0), (b_ada, 2), (b_ada, 8)):
                        eng.tensor_scalar(b[:, lo:lo + 2], b[:, lo:lo + 2], 1.0, None, ALU.add).then_inc(s_fix2, 1)
                    eng.wait_ge(s_fix2, 3)
                    eng.wait_ge(s_mod, 2)
                    for slot, (dst, b, lo, norm_w) in enumerate((
                            (scale0m, b_film2, 0, n2), (shift0m, b_film2, 2, None),
                            (shift1a, b_ada, 0, None), (scale1a, b_ada, 2, None),
                            (shift1m, b_ada, 6, None), (scale1m, b_ada, 8, None))):
                        ins = add_bias(eng, pmod, 2 * slot, dst, b, lo, norm_w)
                    ins.then_inc(s_fix2, 1)

                q_hi, q_lo = sb("q_hi", [P, KT * S], F32R), sb("q_lo", [P, KT * S], F32R)
                v_hi = [sb(f"v_hi{u}", [P, TH * D], F32R) for u in range(UNROLL)]
                v_lo = [sb(f"v_lo{u}", [P, TH * D], F32R) for u in range(UNROLL)]
                probs = [sb(f"probs{u}", [P, TH * S]) for u in range(UNROLL)]
                negmax = sb("negmax", [P, TH])
                psums = [sb(f"psums{u}", [P, TH]) for u in range(UNROLL)]
                prec = sb("prec", [P, TH])
                pT_hi, pT_lo = sb("pT_hi", [P, TH * S], F32R), sb("pT_lo", [P, TH * S], F32R)
                orow_bc = [sb(f"orow_bc{u}", [P, D]) for u in range(UNROLL)]
                s_row = [sem(f"row{u}") for u in range(UNROLL)]
                xb = [sb(f"xb{u}", [P, TH * D]) for u in range(UNROLL)]
                e_q, e_v, e_s, e_pT, e_av = (event(n) for n in ("q", "v", "s1", "pT", "av1"))
                e_hi = {n: event("hi_" + n) for n in ("q", "v", "p")}
                e_lo = {n: event("lo_" + n) for n in ("q", "v", "p")}
                e_max, e_exp, e_rec = (event(n) for n in ("max1", "exp1", "rec"))
                e_xb, e_res = event("xb"), event("res")
                norm = Norm(sb, event, True, scale0a, bT, (e_s, 1))

                T_PE = {"T": 22, "S": 39, "AV": 58, "q": 30, "v": 33, "pT": 52.5}
                T_ACT = {"xhat": 9.5, "hi_h": 23.5, "hi_q": 33.5, "hi_v": 37, "exp": 45, "hi_p": 54.5}
                T_DVE = {"stats": 0.5, "lo_h": 25.5, "lo_q": 35.5, "lo_v": 38, "max": 43.5, "lo_p": 55, "res": 62}
                T_POOL = {"root": 3, "xb": 50}
                T_SP = {"row": 30}
                EARLY = 0

                with nc.Block() as blk:
                    @blk.tensor
                    def _(eng):
                        def q_proj(b):
                            norm.e_lo.wait(eng, b)
                            e_lo["q"].wait(eng, b.back(1))
                            for t in range(KT):
                                c = [slice(k * D + t * P, k * D + (t + 1) * P) for k in range(KT)]
                                ins = mm3(eng, bQ[:, t * S:(t + 1) * S],
                                          [((m_hi[:, c[k]], m_lo[:, c[k]]), norm.tokens(b, k)) for k in range(KT)])
                            e_q.by(ins)

                        def v_proj(b):
                            norm.e_lo.wait(eng, b)
                            e_lo["v"].wait(eng, b.back(1))
                            for h in range(TH):
                                ins = mm3(eng, bV[:, h * D:(h + 1) * D],
                                          [(norm.tokens(b, k, h), (vp_hi[:, k * D:(k + 1) * D], vp_lo[:, k * D:(k + 1) * D]))
                                           for k in range(KT)])
                            e_v.by(ins)

                        def transpose_x(b):
                            norm.e_lo.wait(eng, b.back(1))
                            norm.transpose(eng, b)

                        def scores(b):
                            e_lo["q"].wait(eng, b)
                            e_exp.wait(eng, b.back(1))
                            for qh in range(TH):
                                c = [slice(t * S + qh * P, t * S + (qh + 1) * P) for t in range(KT)]
                                ins = mm3(eng, bS[:, qh * S:(qh + 1) * S],
                                          [((q_hi[:, c[t]], q_lo[:, c[t]]), norm.tokens(b, t)) for t in range(KT)])
                            e_s.by(ins)

                        def transpose_p(b):
                            e_exp.wait(eng, b)
                            e_lo["p"].wait(eng, b.back(1))
                            for kh in range(TH):
                                for qh in range(TH):
                                    ins = eng.transpose(bPT[:, kh * S + qh * P:kh * S + (qh + 1) * P],
                                                        probs[b.par][:, qh * S + kh * P:qh * S + (kh + 1) * P], ident[:, :])
                            e_pT.by(ins)

                        def attend(b):
                            e_lo["p"].wait(eng, b)
                            e_lo["v"].wait(eng, b)
                            e_res.wait(eng, b.back(1))
                            for qh in range(TH):
                                cols = [slice(kh * S + qh * P, kh * S + (qh + 1) * P) for kh in range(TH)]
                                ins = mm3(eng, bR[:, qh * D:(qh + 1) * D], [
                                    ((pT_hi[:, cols[kh]], pT_lo[:, cols[kh]]),
                                     (v_hi[b.par][:, kh * D:(kh + 1) * D], v_lo[b.par][:, kh * D:(kh + 1) * D]))
                                    for kh in range(TH)])
                            e_av.by(ins)

                        run_tasks(eng, schedule(EARLY, T_PE, LATE_PE), {
                            "film2": lambda b: film2_products(eng), "ada0": lambda b: ada_products(eng, (0, 1, 2, 3), 4),
                            "ada1": lambda b: ada_products(eng, (6, 7, 8, 9), 8), "gates": lambda b: gate_products(eng),
                            "T": transpose_x, "q": q_proj, "v": v_proj, "S": scores,
                            "pT": transpose_p, "AV": attend}, once=LATE_PE)

                    @blk.scalar
                    def _(eng):
                        def hi_q(b):
                            e_q.wait(eng, b)
                            e_s.wait(eng, b.back(1))
                            for t in range(KT):
                                c = slice(t * S, (t + 1) * S)
                                ins = eng.activation(q_hi[:, c], bQ[:, c], ACT.Identity, bias=per_seq(biasq, t, b))
                            e_hi["q"].by(ins)

                        def hi_plain(b, name, bk, dst, e_in, buffers):
                            e_in.wait(eng, b)
                            e_av.wait(eng, b.back(buffers))
                            e_hi[name].by(eng.activation(dst[:, :], bk[:, :], ACT.Copy))

                        def exp(b):
                            e_max.wait(eng, b)
                            e_pT.wait(eng, b.back(UNROLL))
                            e_rec.wait(eng, b.back(UNROLL))
                            for h in range(TH):
                                ins = eng.activation(probs[b.par][:, h * S:(h + 1) * S], bS[:, h * S:(h + 1) * S], ACT.Exp,
                                                     bias=negmax[:, h:h + 1], accum_out=psums[b.par][:, h:h + 1])
                            e_exp.by(ins)

                        run_tasks(eng, schedule(EARLY, T_ACT), {
                            "xhat": lambda b: norm.normalize(eng, b), "hi_h": lambda b: norm.evac_hi(eng, b),
                            "hi_q": hi_q,
                            "hi_v": lambda b: hi_plain(b, "v", bV, v_hi[b.par], e_v, UNROLL), "exp": exp,
                            "hi_p": lambda b: hi_plain(b, "p", bPT, pT_hi, e_pT, 1)})

                    @blk.vector
                    def _(eng):
                        def low_q(b):
                            e_hi["q"].wait(eng, b)
                            for t in range(KT):
                                c = slice(t * S, (t + 1) * S)
                                ins = eng.scalar_tensor_tensor(out=q_lo[:, c], in0=bQ[:, c], scalar=per_seq(biasq, t, b),
                                                               in1=q_hi[:, c].bitcast(F32), op0=ALU.add, op1=ALU.subtract)
                            e_lo["q"].by(ins)

                        def lo_plain(b, name, bk, hi, lo):
                            e_hi[name].wait(eng, b)
                            e_lo[name].by(eng.tensor_tensor(lo[:, :], bk[:, :], hi[:, :].bitcast(F32), ALU.subtract))

                        def maximum(b):
                            e_s.wait(eng, b)
                            e_exp.wait(eng, b.back(1))
                            e_max.by(eng.tensor_reduce(negmax[:, :], bS[:, :].rearrange("p (h k) -> p h k", h=TH),
                                                       AX, ALU.max, negate=True))

                        def residual(b):
                            e_exp.wait(eng, b)
                            e_res.wait(eng, b.back(1))
                            e_rec.by(eng.reciprocal(prec[:, :], psums[b.par][:, :]))
                            e_rec.wait(eng, b)
                            e_xb.wait(eng, b)
                            e_av.wait(eng, b)
                            for h in range(TH):
                                c = slice(h * D, (h + 1) * D)
                                ins = eng.scalar_tensor_tensor(out=x_at(b)[:, h], in0=bR[:, c], scalar=prec[:, h:h + 1],
                                                               in1=xb[b.par][:, c], op0=ALU.mult, op1=ALU.add)
                            e_res.by(ins)

                        run_tasks(eng, schedule(EARLY, T_DVE, LATE_DVE), {
                            "modulation": lambda b: late_modulation(eng),
                            "stats": lambda b: norm.stats(eng, b, x_in), "lo_h": lambda b: norm.evac_lo(eng, b),
                            "lo_q": low_q,
                            "lo_v": lambda b: lo_plain(b, "v", bV, v_hi[b.par], v_lo[b.par]), "max": maximum,
                            "lo_p": lambda b: lo_plain(b, "p", bPT, pT_hi, pT_lo), "res": residual},
                                  once=LATE_DVE)
                        eng.wait_ge(s_gate, 1)
                        eng.tensor_tensor(gates[:, :], pmod[0:NB, :], b_gate[:, :], ALU.add)

                    @blk.gpsimd
                    def _(eng):
                        def add_bias(b):
                            e_res.wait(eng, b.back(UNROLL))
                            eng.wait_ge(s_row[b.par], (b.pair + 1) * 16)
                            for h in range(TH):
                                ins = eng.tensor_tensor(xb[b.par][:, h * D:(h + 1) * D], x_at(b)[:, h],
                                                        orow_bc[b.par][:, :], ALU.add)
                            e_xb.by(ins)
                        run_tasks(eng, schedule(EARLY, T_POOL), {"root": lambda b: norm.root(eng, b), "xb": add_bias})

                    @blk.sync
                    def _(eng):
                        rd = mod_dram[2].rearrange("(j u) n -> j u n", u=UNROLL)

                        def load_row(b):
                            e_xb.wait(eng, b.back(UNROLL))
                            eng.dma_start(orow_bc[b.par][:, :], rd[b.pair, b.par, 0:D].partition_broadcast(P))\
                               .then_inc(s_row[b.par], 16)
                        def load_ada(b):
                            eng.dma_start(w_ada[:, :].rearrange("p (t n) -> p t n", t=KT),
                                          a["L1_cond_w_ada"].rearrange("(t p) n -> p t n", p=P)).then_inc(s_ada, 16)

                        def late_loads(b):
                            n = (NB - PEEL) // X_REST
                            for c in range(X_REST):
                                load_x(eng, PEEL + c * n, n, x_in[1][0])
                            preload(eng, staged["B"].values())

                        run_tasks(eng, schedule(EARLY, T_SP, LATE_SP), {
                            "row": load_row, "ada": load_ada, "late loads": late_loads}, once=LATE_SP)

        def phase_mlp(layer):
            l1 = layer == 1
            with ExitStack() as st:
                sb, ps, sem, event = allocator(st, "BD"[layer] + "_")
                hbank, tbank, obank = banks[:4], banks[4], banks[5:7]
                bias1 = sb("bias1", [P, HT * NB])
                gate_row = sb("gate_row", [NB, 2 * D]) if l1 else None
                bias2 = None if l1 else sb("bias2", [P, D])
                w1n, w2n, b1n, b2n = (("L1_cond_w_mlp1", "L1_cond_w_mlp2", "L1_cond_b_mlp1", "L1_cond_b_mlp2") if l1 else
                                      ("L0_cond_mlp_w1", "L0_cond_mlp_w2", "L0_cond_mlp_b1", "L0_cond_mlp_b2"))
                held = hold_weights(sb, [("w1", a[w1n]), ("w2", a[w2n])])
                ws = load_weights(sem, held, {k: (raw(e), e[2]) for k, e in staged["BD"[layer]].items()})
                bcol = sb("bcol", [P, HT])
                b2row = sb("b2row", [NB, D]) if l1 else None
                s_b, s_b2, s_mm, s_g, s_low1, s_low2, s_bias1 = (
                    sem(n) for n in ("b", "b2", "mm", "g", "low1", "low2", "bias1"))
                pshift = banks[7]

                def emit_hi(eng, key):
                    w, hi, _, _, _, _, s_in, s_sp = ws[key]
                    eng.wait_ge(s_in, 16)
                    eng.activation(hi[:, :], w[:, :], ACT.Copy).then_inc(s_sp, 1)

                def emit_lo(eng, key):
                    w, hi, lo, _, _, _, _, s_sp = ws[key]
                    eng.wait_ge(s_sp, 1)
                    return eng.tensor_tensor(lo[:, :], w[:, :], hi[:, :].bitcast(F32), ALU.subtract)

                g = [sb(f"g{u}", [P, 2 * S]) for u in range(4)]
                g_hi = [sb(f"g_hi{u}", [P, 2 * S], F32R) for u in range(4)]
                g_lo = [sb(f"g_lo{u}", [P, 2 * S], F32R) for u in range(4)]
                xb = [sb(f"xb{u}", [P, TH * D]) for u in range(UNROLL)]
                gbc = [sb(f"gbc{u}", [P, 2 * D]) for u in range(UNROLL)] if l1 else None
                tmp = sb("tmp", [P, TH * D]) if l1 else None
                e_mm1, e_gelu, e_ghi, e_glo, e_mm2 = (event(n, 4) for n in ("mm1", "gelu", "ghi", "glo", "mm2"))
                e_res, e_xb = event("res"), event("xb")
                e_tmp = event("tmp") if l1 else None
                s_gin = [sem(f"gin{u}") for u in range(UNROLL)]
                s_out = [sem(f"out{u}") for u in range(UNROLL)]
                norm = Norm(sb, event, not l1, scale1m if l1 else scale0m, tbank, (e_mm1, 4))
                func = ACT.Gelu_apprx_tanh if l1 else ACT.Gelu

                with nc.Block() as blk:
                    @blk.tensor
                    def _(eng):
                        for t in range(HT):
                            ins = shift_bias(eng, pshift, t * NB, ws["w1"], t * P, shift1m if l1 else shift0m)
                        ins.then_inc(s_mm, 1)

                        def first(b, u):
                            return b.reg is None and b.off == 0 and u == 0

                        def up(b, u):
                            if not b.exists(NB):
                                return
                            if first(b, u):
                                eng.wait_ge(s_low1, 1)
                            if u == 0:
                                norm.e_lo.wait(eng, b)
                            e_gelu.wait(eng, b.back(1), u + 1)
                            for d in range(2):
                                ins = mm3(eng, hbank[u][:, d * S:(d + 1) * S],
                                          [(weight(ws["w1"], k, (2 * u + d) * P, P), norm.tokens(b, k)) for k in range(KT)])
                            e_mm1.by(ins)

                        def down(b, u):
                            if not b.exists(NB):
                                return
                            if first(b, u):
                                eng.wait_ge(s_low2, 1)
                            e_glo.wait(eng, b, u + 1)
                            if u == 0:
                                e_res.wait(eng, b.back(UNROLL))
                            for h in range(TH):
                                for d in range(2):
                                    c = slice(d * S + h * P, d * S + (h + 1) * P)
                                    ins = mm3(eng, obank[b.par][:, h * D:(h + 1) * D],
                                              [((g_hi[u][:, c], g_lo[u][:, c]), weight(ws["w2"], 2 * u + d, 0, D))],
                                              start=u == 0 and h == 0 and d == 0, stop=u == 3 and d == 1, skip=True)
                            e_mm2.by(ins)

                        def it(i):
                            f, m, r = i, i.back(1), i.back(2)
                            up(m, 0)
                            down(r, 3)
                            up(m, 1)
                            down(m, 0)
                            up(m, 2)
                            down(m, 1)
                            if f.exists(NB):
                                norm.e_lo.wait(eng, f.back(1))
                                norm.transpose(eng, f)
                            up(m, 3)
                            down(m, 2)
                        run_pipeline(eng, NB, 2, it)

                    @blk.scalar
                    def _(eng):
                        def gelu(b, u):
                            if not b.exists(NB):
                                return
                            e_mm1.wait(eng, b, u + 1)
                            if b.reg is None and b.off == 0 and u == 0:
                                eng.wait_ge(s_bias1, 1)
                            e_glo.wait(eng, b.back(1), u + 1)
                            for d in range(2):
                                ins = eng.activation(g[u][:, d * S:(d + 1) * S], hbank[u][:, d * S:(d + 1) * S], func,
                                                     bias=per_seq(bias1, 2 * u + d, b))
                            e_gelu.by(ins)

                        emit_hi(eng, "w1")

                        def it(i):
                            f, m = i, i.back(1)
                            if i.reg is None and i.off == 0:
                                norm.evac_hi(eng, f)
                                emit_hi(eng, "w2")
                                return
                            for u in range(3):
                                gelu(m, u)
                            if f.exists(NB):
                                norm.evac_hi(eng, f)
                            gelu(m, 3)
                        run_pipeline(eng, NB, 2, it)

                    @blk.vector
                    def _(eng):
                        def split(b, u):
                            if not b.exists(NB):
                                return
                            e_gelu.wait(eng, b, u + 1)
                            e_mm2.wait(eng, b.back(1), u + 1)
                            e_ghi.by(eng.tensor_copy(g_hi[u][:, :], g[u][:, :]))
                            e_ghi.wait(eng, b, u + 1)
                            e_glo.by(eng.tensor_tensor(g_lo[u][:, :], g[u][:, :], g_hi[u][:, :].bitcast(F32), ALU.subtract))

                        def weights(eng):
                            emit_lo(eng, "w1").then_inc(s_low1, 1)
                            norm.evac_lo(eng, Seq(None, 0))
                            eng.wait_ge(s_b, 16)
                            eng.wait_ge(s_mm, 1)
                            for t in range(HT):
                                ins = eng.tensor_scalar(bias1[:, t * NB:(t + 1) * NB], pshift[:, t * NB:(t + 1) * NB],
                                                        bcol[:, t:t + 1], None, ALU.add)
                            ins.then_inc(s_bias1, 1)
                            if l1:
                                eng.tensor_copy(gate_row[:, 0:D], gates[:, D:2 * D]).then_inc(s_g, 1)
                                eng.wait_ge(s_b2, 16)
                                eng.tensor_tensor(gate_row[:, D:2 * D], gates[:, D:2 * D], b2row[:, :], ALU.mult).then_inc(s_g, 1)

                        def it(i):
                            f, m, r = i, i.back(1), i.back(2)
                            if f.exists(NB):
                                norm.stats(eng, f)
                            if i.reg is None and i.off == 0:
                                norm.normalize(eng, f)
                                weights(eng)
                                return
                            split(m, 0)
                            if r.exists(NB):
                                e_mm2.wait(eng, r)
                                e_xb.wait(eng, r)
                                o3 = obank[r.par][:, :].rearrange("p (h n) -> p h n", h=TH)
                                x3 = xb[r.par][:, :].rearrange("p (h n) -> p h n", h=TH)
                                if l1:
                                    e_res.wait(eng, r.back(1))
                                    t3 = tmp[:, :].rearrange("p (h n) -> p h n", h=TH)
                                    for h in range(TH):
                                        ins = eng.tensor_tensor(t3[:, h], o3[:, h], gbc[r.par][:, 0:D], ALU.mult)
                                    e_tmp.by(ins)
                                    e_tmp.wait(eng, r)
                                    e_res.by(eng.tensor_tensor(x_at(r), t3, x3, ALU.add))
                                else:
                                    e_res.by(eng.tensor_tensor(x_at(r), o3, x3, ALU.add))
                            split(m, 1)
                            if f.exists(NB):
                                norm.normalize(eng, f)
                            split(m, 2)
                            if f.exists(NB):
                                norm.evac_lo(eng, f)
                            split(m, 3)
                        run_pipeline(eng, NB, 2, it)

                    @blk.gpsimd
                    def _(eng):
                        def it(i):
                            if i.exists(NB):
                                norm.root(eng, i)
                            if i.reg is None and i.off == 0:
                                emit_lo(eng, "w2").then_inc(s_low2, 1)
                                if not l1:
                                    eng.wait_ge(s_b2, 16)
                            m = i.back(1)
                            if m.exists(NB):
                                e_res.wait(eng, m.back(UNROLL))
                                if l1:
                                    eng.wait_ge(s_gin[m.par], (m.pair + 1) * 16)
                                for h in range(TH):
                                    ins = eng.tensor_tensor(xb[m.par][:, h * D:(h + 1) * D], x_at(m)[:, h],
                                                            gbc[m.par][:, D:2 * D] if l1 else bias2[:, :], ALU.add)
                                e_xb.by(ins)
                        run_pipeline(eng, NB, 2, it)

                    def load_biases(eng):
                        with nc.allow_non_contiguous_dma(reason="bias vectors, one element per partition"):
                            eng.dma_start(bcol[:, :], a[b1n].rearrange("(t p) -> p t", p=P)).then_inc(s_b, 16)
                        eng.dma_start((b2row if l1 else bias2)[:, :], a[b2n].partition_broadcast(NB if l1 else P))\
                           .then_inc(s_b2, 16)

                    if not l1:
                        @blk.sync
                        def _(eng):
                            load_biases(eng)
                            eng.wait_ge(s_mm, 1)
                            eng.wait_ge(s_low1, 1)
                            preload(eng, staged["C"].values())
                    else:
                        @blk.sync
                        def _(eng):
                            preload(eng, [staged["D"]["w2"]])
                            load_biases(eng)
                            eng.wait_ge(s_g, 2)
                            eng.dma_start(mod_dram[1], gate_row[:, :]).then_inc(s_g, 16)
                            eng.wait_ge(s_g, 2 + 16)
                            gd = mod_dram[1].rearrange("(j u) n -> j u n", u=UNROLL)
                            od = out.rearrange("(j u) (h p) n -> j u p h n", u=UNROLL, p=P)

                            def it(i):
                                f, r = i, i.back(2)
                                if f.exists(NB):
                                    e_res.wait(eng, f.back(UNROLL))
                                    eng.dma_start(gbc[f.par][:, :], gd[f.pair, f.par].partition_broadcast(P))\
                                       .then_inc(s_gin[f.par], 16)
                                if r.exists(NB):
                                    e_res.wait(eng, r)
                                    eng.dma_start(od[r.pair, r.par], x_at(r)).then_inc(s_out[r.par], 16)
                            run_pipeline(eng, NB, 2, it)
                            for s in s_out:
                                eng.wait_ge(s, NB // UNROLL * 16)

        def phase_l1_attention():
            with ExitStack() as st:
                sb, ps, sem, event = allocator(st, "C_")
                sbank = banks[:2]
                stbank = banks[2:4]
                ybank, misc = banks[4], banks[5:8]
                bias_q, bias_k = sb("bias_q", [P, KT * NB]), sb("bias_k", [P, KT * NB])
                NT = NH // 2
                HALF = P // 2
                ROW_HI, ROW_LO = 3 * CH, 3 * CH + 1
                assert NH * CH == D
                MAX_DMAS = 2
                K_SLOTS = ("hi", "lo", "hi")
                K_DMAS = 2 * len(K_SLOTS)
                kx = [[sb(f"kx{u}{e}", [P, NT * S], F32R) for e in range(2)] for u in range(UNROLL)]
                one_rows = [sb(f"ones{e}", [P, 1]) for e in range(2)]
                s_m, s_kx = sem("m"), sem("kx")
                wk_hi, wk_lo = sb("wk_hi", [P, KT * D], F32R), sb("wk_lo", [P, KT * D], F32R)
                vaug = [sb(f"vaug{u}", [P, TH * NH * 32]) for u in range(UNROLL)]
                held = hold_weights(sb, [(n, a["L1_cond_w_qkv"][:, c:c + D]) for n, c in (("q", D), ("v", 2 * D))] +
                                    [("proj", a["L1_cond_w_proj"])])
                with ExitStack() as pre:
                    psb, _, psem, _ = allocator(pre, "Cp_")
                    ws = load_weights(psem, held, {k: (raw(e), e[2]) for k, e in staged["C"].items()})
                    wk_raw, s_wk = raw(staged["C"]["k"]), staged["C"]["k"][2]
                    cv = psb("cv", [P, KT * NB])
                    brow, gate_row = psb("brow", [NB, D]), psb("gate_row", [NB, 2 * D])
                    wk = psb("wk", [P, KT * D])
                    s_kp, s_kh, s_mmk = psem("kp"), psem("kh"), psem("mmk")
                    pshift = banks[0], banks[1], banks[2]
                    s_b, s_mm, s_mmv, s_cv, s_pj, s_g = (psem(n) for n in ("b", "mm", "mmv", "cv", "pj", "g"))
                    with nc.Block() as blk:
                        @blk.sync
                        def _(eng):
                            eng.dma_start(brow[:, :], a["L1_cond_b_proj"].partition_broadcast(NB)).then_inc(s_b, 16)
                            eng.wait_ge(s_g, 3)
                            eng.dma_start(mod_dram[0], gate_row[:, :]).then_inc(s_b, 16)
                            eng.wait_ge(s_b, 32)

                        @blk.scalar
                        def _(eng):
                            emit_hi(eng, ws)
                            eng.wait_ge(s_kp, 1)
                            eng.activation(wk_hi[:, :], wk[:, :], ACT.Copy).then_inc(s_kh, 1)

                        @blk.gpsimd
                        def _(eng):
                            for u in range(UNROLL):
                                v4 = vaug[u][:, :].rearrange("p (k h c) -> p k h c", k=TH, c=32)
                                eng.memset(v4[:, :, :, CH:32], 1.0)
                            for e in range(2):
                                eng.memset(one_rows[e][:, :], 1.0).then_inc(s_m, 1)
                            eng.wait_ge(s_m, 2)
                            for e in range(2):
                                eng.affine_select(out=one_rows[e][:, :], in_=one_rows[e][:, :], compare_op=ALU.is_ge,
                                                  fill=0.0, base=-(e * HALF + ROW_HI), pattern=[[0, 1]],
                                                  channel_multiplier=1).then_inc(s_m, 1)
                            eng.wait_ge(s_m, 4)
                            for e in range(2):
                                eng.affine_select(out=one_rows[e][:, :], in_=one_rows[e][:, :], compare_op=ALU.is_ge,
                                                  fill=0.0, base=e * HALF + ROW_LO, pattern=[[0, 1]],
                                                  channel_multiplier=-1).then_inc(s_m, 1)

                        @blk.tensor
                        def _(eng):
                            for i, n, s_done in ((2, "v", s_mmv), (0, "q", s_mm)):
                                for t in range(KT):
                                    ins = shift_bias(eng, pshift[i], t * NB, ws[n], t * P, shift1a)
                                ins.then_inc(s_done, 1)
                            eng.wait_ge(s_cv, 1)
                            w, _, _, t, N, _, s_in, _ = ws["proj"]
                            eng.wait_ge(s_in, 16)
                            for k in range(KT):
                                ins = eng.matmul(misc[1][0:NB, 0:D], cv[:, k * NB:(k + 1) * NB], w[:, k * N:(k + 1) * N],
                                                 start=k == 0, stop=k == KT - 1)
                            ins.then_inc(s_pj, 1)
                            eng.wait_ge(s_kp, 1)
                            for t in range(KT):
                                for k in range(KT):
                                    ins = eng.matmul(pshift[1][:, t * NB:(t + 1) * NB],
                                                     wk[:, k * D + t * P:k * D + (t + 1) * P],
                                                     shift1a[:, k * NB:(k + 1) * NB], start=k == 0, stop=k == KT - 1)
                            ins.then_inc(s_mmk, 1)

                        @blk.vector
                        def _(eng):
                            eng.wait_ge(s_wk, 16)
                            for k in range(KT):
                                for e in range(2):
                                    d4 = wk[:, k * D + e * P:k * D + (e + 1) * P].rearrange("p (w c t) -> p w c t", w=2, c=CH)
                                    s5 = wk_raw[:, k * D:(k + 1) * D].rearrange("p (w t e c) -> p w c t e", w=2, e=2, c=CH)
                                    ins = eng.tensor_copy(d4, s5[:, :, :, :, e])
                            ins.then_inc(s_kp, 1)
                            def from_bank(dst, i):
                                return eng.tensor_copy(dst[:, :], pshift[i][:, 0:KT * NB])

                            eng.wait_ge(s_mmv, 1)
                            from_bank(cv, 2).then_inc(s_cv, 1)
                            eng.wait_ge(s_b, 16)
                            eng.tensor_copy(gate_row[:, 0:D], gates[:, 0:D]).then_inc(s_g, 1)
                            eng.wait_ge(s_pj, 1)
                            eng.tensor_tensor(brow[:, :], misc[1][0:NB, 0:D], brow[:, :], ALU.add).then_inc(s_g, 1)
                            eng.wait_ge(s_g, 2)
                            eng.tensor_tensor(gate_row[:, D:2 * D], gates[:, 0:D], brow[:, :], ALU.mult).then_inc(s_g, 1)
                            emit_lo(eng, ws)
                            eng.wait_ge(s_kh, 1)
                            eng.tensor_tensor(wk_lo[:, :], wk[:, :], wk_hi[:, :].bitcast(F32), ALU.subtract)
                            eng.wait_ge(s_mm, 1)
                            from_bank(bias_q, 0)
                            eng.wait_ge(s_mmk, 1)
                            from_bank(bias_k, 1)

                qk = {n: sb(n, [P, KT * S], F32R) for n in ("q_hi", "q_lo", "k_hi", "k_lo")}
                qs = [sb(f"qs{u}", [P, NT * S], F32R) for u in range(UNROLL)]
                NP = 8
                probs = [sb(f"probs{i}", [P, TH * S]) for i in range(NP)]
                negmax = sb("negmax", [P, TH * NH])
                mhl = [sb(f"mhl{w}", [NH // 2, 2 * S], F32R) for w in range(2)]
                ysb = [sb(f"ysb{w}", [P, 2 * S]) for w in range(2)]
                yrec = sb("yrec", [P, NH])
                ytok = sb("ytok", [P, TH * D])
                y_hi, y_lo = sb("y_hi", [P, KT * S], F32R), sb("y_lo", [P, KT * S], F32R)
                gbc = [sb(f"gbc{u}", [P, 2 * D]) for u in range(UNROLL)]
                tmp = sb("tmp", [P, TH * D])
                e_q, e_k, e_v, e_y2, e_pr = (event(n) for n in ("q", "k", "v", "y2", "pr"))
                e_hiq, e_hik, e_loq, e_lok, e_vev = (event(n) for n in ("hiq", "hik", "loq", "lok", "vev"))
                e_sq, e_sqev = event("sq", 4), event("sqev", 4)
                s_kst = [[sem(f"kst{w}{u}") for u in range(UNROLL)] for w in range(2)]
                e_s, e_max, e_st, e_exp = (event(n, NH) for n in ("s", "max", "st", "exp"))
                e_mT, e_mhi, e_mlo = (event(n, 2) for n in ("mT", "mhi", "mlo"))
                s_mdma = [[sem(f"mdma{w}{u}") for u in range(UNROLL)] for w in range(2)]
                e_av = event("av", 4)
                e_ysb, e_y1, e_yrec, e_ytok = (event(n, 2) for n in ("ysb", "y1", "yrec", "ytok"))
                e_yhi, e_ylo = event("yhi"), event("ylo")
                e_xb, e_tmp, e_res = event("xb"), event("tmp"), event("res")
                s_gin = [sem(f"gin{u}") for u in range(UNROLL)]
                scl = 1.0 / CH

                T_PE = {"T": -0.5, "q": 3, "k": 6.5, "v": 16.5, "SQ0": 8.5, "SQ1": 12, "SQ2": 13, "SQ3": 14.5,
                        "M0": 25.5, "M1": 33, "AV0": 38, "AV1": 41, "AV2": 46.5, "AV3": 49.5, "Y1a": 45, "Y1b": 52,
                        "Y2": 55, "PR": 59}
                T_ACT = {"hi_h": 0.5, "hi_q": 3.5, "hi_k": 6.5, "v": 18, "SQ0": 8, "SQ1": 12.5, "SQ2": 14,
                         "SQ3": 15.5, "M0": 25.5, "M1": 32.5, "Y0": 42, "Y1": 50, "hi_y": 56}
                T_DVE = {"stats": -3.5, "xhat": -2, "lo_h": 1.5, "lo_q": 4.5, "lo_k": 7.5, "M0": 26, "M1": 33.5,
                         "Y1a": 46, "Y1b": 53.5, "lo_y": 57, "out": 59.5}
                EARLY = 4
                T_S, T_ST = {h: 16 + h for h in range(NH)}, {h: 32.5 + h for h in range(NH)}

                pe_order = schedule(EARLY, T_S, {f"ST{h}": t for h, t in T_ST.items()}, T_PE)

                ring = [(k, n) for k, n in pe_order if n in T_PE and not n.startswith("AV")]
                names = [n for _, n in ring]

                def mbank(name):
                    return misc[names.index(name) % 3]

                norm = Norm(sb, event, False, scale1a, mbank("T"), (e_v, 1))
                freed = {"M0": (e_mlo, 1), "M1": (e_mlo, 2), "v": (e_vev, 1), "Y1a": (e_ytok, 1), "Y1b": (e_ytok, 2),
                         "T": (norm.e_lo, 1), "Y2": (e_ylo, 1), "q": (e_loq, 1), "k": (e_lok, 1), "PR": (e_tmp, 1)}
                freed.update({f"SQ{u}": (e_sqev, u + 1) for u in range(4)})

                def bank_free(eng, name, b):
                    mine = [(k, n) for k, n in ring if mbank(n) is mbank(name)]
                    at = [n for _, n in mine].index(name)
                    i = Seq(b.reg, b.off + mine[at][0])
                    while not i.before_first():
                        at -= 1
                        if at < 0:
                            at, i = len(mine) - 1, i.back(1)
                        k, prev = mine[at]
                        if i.back(k).exists(NB):
                            ev, count = freed[prev]
                            ev.wait(eng, i.back(k), count)
                            return

                with nc.Block() as blk:
                    @blk.tensor
                    def _(eng):
                        def scores(b, h):
                            t, e = divmod(h, 2)
                            if h % 4 == 0:
                                e_sqev.wait(eng, b, h // 4 + 1)
                            if h % 8 == 0:
                                eng.wait_ge(s_kst[h // 8][b.par], (b.pair + 1) * K_DMAS * 16)
                            e_max.wait(eng, b, h - 1)
                            for qh in range(TH):
                                ins = eng.matmul(sbank[h % 2][:, qh * S:(qh + 1) * S],
                                                 qs[b.par][:, t * S + qh * P:t * S + (qh + 1) * P],
                                                 kx[b.par][e][:, t * S:(t + 1) * S], start=True, stop=True)
                            e_s.by(ins)

                        def scores_t(b, h):
                            t, e = divmod(h, 2)
                            if h % 8 == 0:
                                eng.wait_ge(s_mdma[h // 8][b.par], (b.pair + 1) * MAX_DMAS * 16)
                            e_exp.wait(eng, b, h - 1)
                            for kh in range(TH):
                                ins = eng.matmul(stbank[h % 2][:, kh * S:(kh + 1) * S],
                                                 kx[b.par][e][:, t * S + kh * P:t * S + (kh + 1) * P],
                                                 qs[b.par][:, t * S:(t + 1) * S], start=True, stop=True)
                            e_st.by(ins)

                        def weighted_v(b, g):
                            e_exp.wait(eng, b, 4 * g + 4)
                            if g == 0:
                                e_vev.wait(eng, b)
                                e_ysb.wait(eng, b.back(1), 2)
                            if g == 2:
                                e_ysb.wait(eng, b, 1)
                            for kh in range(TH):
                                for j in range(4):
                                    h = 4 * g + j
                                    v0 = (kh * NH + h) * 32
                                    ins = eng.matmul(ybank[32 * j:32 * j + 32, (g % 2) * S:(g % 2 + 1) * S],
                                                     vaug[b.par][:, v0:v0 + 32], probs[h % NP][:, kh * S:(kh + 1) * S],
                                                     start=kh == 0, stop=kh == TH - 1, skip_group_check=True)
                            e_av.by(ins)

                        def max_t(b, w):
                            e_max.wait(eng, b, 8 * w + 8)
                            for qh in range(TH):
                                ins = eng.transpose(mbank(f"M{w}")[0:NH // 2, qh * P:(qh + 1) * P],
                                                    negmax[:, qh * NH + 8 * w:qh * NH + 8 * w + 8], ident[:, :])
                            e_mT.by(ins)

                        def y_tok(b, w):
                            e_ysb.wait(eng, b, w + 1)
                            for qh in range(TH):
                                for g in range(2):
                                    c = (qh * 2 + g) * P
                                    ins = eng.transpose(mbank("Y1" + "ab"[w])[:, c:c + P],
                                                        ysb[w][:, g * S + qh * P:g * S + (qh + 1) * P], ident[:, :])
                            e_y1.by(ins)

                        def y_chan(b):
                            e_ytok.wait(eng, b)
                            for t in range(KT):
                                for h in range(TH):
                                    ins = eng.transpose(mbank("Y2")[:, t * S + h * P:t * S + (h + 1) * P],
                                                        ytok[:, h * D + t * P:h * D + (t + 1) * P], ident[:, :])
                            e_y2.by(ins)

                        def project(b):
                            e_ylo.wait(eng, b)
                            for h in range(TH):
                                ins = mm3(eng, mbank("PR")[:, h * D:(h + 1) * D], [
                                    ((y_hi[:, t * S + h * P:t * S + (h + 1) * P],
                                      y_lo[:, t * S + h * P:t * S + (h + 1) * P]),
                                     weight(ws["proj"], t, 0, D)) for t in range(KT)])
                            e_pr.by(ins)

                        def qk_cm(b, name, w_hi, w_lo, done):
                            norm.e_lo.wait(eng, b)
                            for t in range(KT):
                                c = [slice(k * D + t * P, k * D + (t + 1) * P) for k in range(KT)]
                                ins = mm3(eng, mbank(name)[:, t * S:(t + 1) * S],
                                          [((w_hi[:, c[k]], w_lo[:, c[k]]), norm.tokens(b, k)) for k in range(KT)])
                            done.by(ins)

                        def v_tok(b):
                            for h in range(TH):
                                ins = mm3(eng, mbank("v")[:, h * D:(h + 1) * D],
                                          [(norm.tokens(b, k, h), weight(ws["v"], k, 0, D)) for k in range(KT)])
                            e_v.by(ins)

                        def stack(b, u):
                            if u == 0:
                                e_loq.wait(eng, b)
                            for d in range(2):
                                t, uu = divmod(2 * u + d, 4)
                                for k, part in enumerate(("hi", "lo")):
                                    ins = eng.matmul(mbank(f"SQ{u}")[:, d * S:(d + 1) * S],
                                                     sel[part][:, uu * P:(uu + 1) * P],
                                                     qk["q_" + part][:, t * S:(t + 1) * S], start=k == 0, stop=k == 1)
                            e_sq.by(ins)

                        tasks = {"T": lambda b: norm.transpose(eng, b),
                                 "q": lambda b: qk_cm(b, "q", ws["q"][1], ws["q"][2], e_q),
                                 "k": lambda b: qk_cm(b, "k", wk_hi, wk_lo, e_k), "v": v_tok,
                                 "M0": lambda b: max_t(b, 0), "M1": lambda b: max_t(b, 1),
                                 "Y1a": lambda b: y_tok(b, 0), "Y1b": lambda b: y_tok(b, 1), "Y2": y_chan, "PR": project}
                        for u in range(4):
                            tasks[f"SQ{u}"] = lambda b, u=u: stack(b, u)
                            tasks[f"AV{u}"] = lambda b, u=u: weighted_v(b, u)
                        for h in range(NH):
                            tasks[h] = lambda b, h=h: scores(b, h)
                            tasks[f"ST{h}"] = lambda b, h=h: scores_t(b, h)

                        run_tasks(eng, pe_order, tasks, lambda name, b: name in names and bank_free(eng, name, b))

                    @blk.scalar
                    def _(eng):
                        def exp(b, h):
                            e_st.wait(eng, b, h + 1)
                            e_av.wait(eng, b if h >= NP else b.back(1), (h - NP) // 4 + 1 if h >= NP else (h + NP) // 4 + 1)
                            e_exp.by(eng.activation(probs[h % NP][:, :], stbank[h % 2][:, :], ACT.Exp, scale=scl))

                        def hi_bias(b, name, dst, bias, e_in, e_out):
                            e_in.wait(eng, b)
                            for t in range(KT):
                                c = slice(t * S, (t + 1) * S)
                                ins = eng.activation(dst[:, c], mbank(name)[:, c], ACT.Identity, bias=per_seq(bias, t, b))
                            e_out.by(ins)

                        def hi_q(b):
                            e_sq.wait(eng, b.back(1))
                            hi_bias(b, "q", qk["q_hi"], bias_q, e_q, e_hiq)

                        def hi_k(b):
                            prev = b.back(1)
                            if not prev.before_first():
                                for w in range(2):
                                    eng.wait_ge(s_kst[w][prev.par], (prev.pair + 1) * K_DMAS * 16)
                            hi_bias(b, "k", qk["k_hi"], bias_k, e_k, e_hik)

                        def stack_q(b, u):
                            e_sq.wait(eng, b, u + 1)
                            e_st.wait(eng, b.back(2), 4 * u + 4)
                            if u == 3:
                                e_lok.wait(eng, b)
                            e_sqev.by(eng.activation(qs[b.par][:, 2 * u * S:(2 * u + 2) * S], mbank(f"SQ{u}")[:, :], ACT.Copy))

                        def max_hi(b, w):
                            e_mT.wait(eng, b, w + 1)
                            prev = b.back(1)
                            if not prev.before_first():
                                eng.wait_ge(s_mdma[w][prev.par], (prev.pair + 1) * MAX_DMAS * 16)
                            e_mhi.by(eng.activation(mhl[w][:, 0:S], mbank(f"M{w}")[0:NH // 2, 0:S], ACT.Copy))

                        def y_out(b, w):
                            e_av.wait(eng, b, 2 * w + 2)
                            e_y1.wait(eng, b.back(1), w + 1)
                            e_ysb.by(eng.activation(ysb[w][:, :], ybank[:, :], ACT.Copy))

                        def hi_y(b):
                            e_y2.wait(eng, b)
                            e_pr.wait(eng, b.back(1))
                            e_yhi.by(eng.activation(y_hi[:, :], mbank("Y2")[:, :], ACT.Copy))

                        def v_out(b):
                            e_v.wait(eng, b)
                            e_av.wait(eng, b.back(2))
                            v4 = vaug[b.par][:, :].rearrange("p (k h c) -> p k h c", k=TH, c=32)
                            s4 = mbank("v")[:, :].rearrange("p (k h c) -> p k h c", k=TH, c=CH)
                            for kh in range(TH):
                                ins = eng.activation(v4[:, kh, :, 0:CH], s4[:, kh], ACT.Copy)
                            e_vev.by(ins)

                        tasks = {"hi_h": lambda b: norm.evac_hi(eng, b), "hi_q": hi_q, "hi_k": hi_k, "v": v_out,
                                 "M0": lambda b: max_hi(b, 0), "M1": lambda b: max_hi(b, 1),
                                 "Y0": lambda b: y_out(b, 0), "Y1": lambda b: y_out(b, 1), "hi_y": hi_y}
                        for u in range(4):
                            tasks[f"SQ{u}"] = lambda b, u=u: stack_q(b, u)
                        for h in range(NH):
                            tasks[h] = lambda b, h=h: exp(b, h)

                        def init_stacks(u):
                            eng.wait_ge(s_m, 6)
                            for e in range(2):
                                ins = eng.activation(kx[u][e][:, :], one_rows[e][:, 0:1].broadcast_to([P, NT * S]), ACT.Copy)
                            ins.then_inc(s_kx, 1)

                        tasks["kx0"], tasks["kx1"] = lambda b: init_stacks(0), lambda b: init_stacks(1)
                        run_tasks(eng, schedule(EARLY, T_ST, T_ACT, {"kx0": 1, "kx1": 17}), tasks, once=("kx0", "kx1"))

                    @blk.vector
                    def _(eng):
                        n3 = negmax[:, :].rearrange("p (q h) -> p q h", q=TH)

                        def maximum(b, h):
                            e_s.wait(eng, b, h + 1)
                            if h % 8 == 0:
                                e_mT.wait(eng, b.back(1), h // 8 + 1)
                            col = h // 8 * 8 + h % 2 * 4 + h % 8 // 2
                            e_max.by(eng.tensor_reduce(n3[:, :, col], sbank[h % 2][:, :].rearrange("p (q k) -> p q k", q=TH),
                                                       AX, ALU.max, negate=True))

                        def max_lo(b, w):
                            e_mhi.wait(eng, b, w + 1)
                            e_mlo.by(eng.tensor_tensor(mhl[w][:, S:2 * S], mbank(f"M{w}")[0:NH // 2, 0:S],
                                                       mhl[w][:, 0:S].bitcast(F32), ALU.subtract))

                        def lo_bias(b, name, hi, lo, bias, e_in, e_out):
                            e_in.wait(eng, b)
                            for t in range(KT):
                                c = slice(t * S, (t + 1) * S)
                                ins = eng.scalar_tensor_tensor(out=lo[:, c], in0=mbank(name)[:, c], scalar=per_seq(bias, t, b),
                                                               in1=hi[:, c].bitcast(F32), op0=ALU.add, op1=ALU.subtract)
                            e_out.by(ins)

                        def lo_k(b):
                            e_st.wait(eng, b.back(2), 8)
                            lo_bias(b, "k", qk["k_hi"], qk["k_lo"], bias_k, e_hik, e_lok)

                        def y_norm(b, w):
                            e_y1.wait(eng, b, w + 1)
                            src = mbank("Y1" + "ab"[w])[:, :].rearrange("p (a c) -> p a c", c=32)
                            if w == 0:
                                e_ytok.wait(eng, b.back(1))
                            else:
                                e_ytok.wait(eng, b, 1)
                            e_yrec.by(eng.reciprocal(yrec[:, :], src[:, :, CH]))
                            e_yrec.wait(eng, b, w + 1)
                            if w == 0:
                                e_y2.wait(eng, b.back(1))
                            for q in range(TH):
                                r3 = yrec[:, q * 8:(q + 1) * 8].unsqueeze(2).broadcast_to([P, 8, CH])
                                o3 = ytok[:, q * D + w * P:q * D + (w + 1) * P].rearrange("p (a c) -> p a c", c=CH)
                                ins = eng.tensor_tensor(o3, src[:, q * 8:(q + 1) * 8, 0:CH], r3, ALU.mult)
                            e_ytok.by(ins)

                        def lo_y(b):
                            e_yhi.wait(eng, b)
                            e_ylo.by(eng.tensor_tensor(y_lo[:, :], mbank("Y2")[:, :], y_hi[:, :].bitcast(F32), ALU.subtract))

                        def gated(b):
                            e_pr.wait(eng, b)
                            e_xb.wait(eng, b)
                            e_res.wait(eng, b.back(1))
                            p3 = mbank("PR")[:, :].rearrange("p (h n) -> p h n", h=TH)
                            t3 = tmp[:, :].rearrange("p (h n) -> p h n", h=TH)
                            for h in range(TH):
                                ins = eng.tensor_tensor(t3[:, h], p3[:, h], gbc[b.par][:, 0:D], ALU.mult)
                            e_tmp.by(ins)

                        tasks = {"stats": lambda b: norm.stats(eng, b), "xhat": lambda b: norm.normalize(eng, b),
                                 "lo_h": lambda b: norm.evac_lo(eng, b),
                                 "lo_q": lambda b: lo_bias(b, "q", qk["q_hi"], qk["q_lo"], bias_q, e_hiq, e_loq),
                                 "lo_k": lo_k, "M0": lambda b: max_lo(b, 0), "M1": lambda b: max_lo(b, 1),
                                 "Y1a": lambda b: y_norm(b, 0), "Y1b": lambda b: y_norm(b, 1), "lo_y": lo_y, "out": gated}
                        for h in range(NH):
                            tasks[h] = lambda b, h=h: maximum(b, h)
                        run_tasks(eng, schedule(EARLY, T_S, T_DVE), tasks)

                    @blk.gpsimd
                    def _(eng):
                        def it(i):
                            r, last = i.back(MAX_SKEW), i.back(MAX_SKEW + 1)
                            if last.exists(NB):
                                e_xb.wait(eng, last)
                                e_tmp.wait(eng, last)
                            if i.exists(NB):
                                norm.root(eng, i)
                            if last.exists(NB):
                                for h in range(TH):
                                    ins = eng.tensor_tensor(x_at(last)[:, h], x_at(last)[:, h], tmp[:, h * D:(h + 1) * D],
                                                            ALU.add)
                                e_res.by(ins)
                            if r.exists(NB):
                                eng.wait_ge(s_gin[r.par], (r.pair + 1) * 16)
                                for h in range(TH):
                                    ins = eng.tensor_tensor(x_at(r)[:, h], x_at(r)[:, h], gbc[r.par][:, D:2 * D], ALU.add)
                                e_xb.by(ins)
                        run_pipeline(eng, NB, MAX_SKEW + 1, it)

                    @blk.sync
                    def _(eng):
                        gd = mod_dram[0].rearrange("(j u) n -> j u n", u=UNROLL)

                        def place_k(b, w):
                            if b.reg is None and b.off < UNROLL:
                                eng.wait_ge(s_kx, b.off + 1)
                            if w == 0:
                                e_lok.wait(eng, b)
                            else:
                                e_sqev.wait(eng, b)
                            for e in range(2):
                                for slot, part in enumerate(K_SLOTS):
                                    row = e * HALF + slot * CH
                                    dst = kx[b.par][e][row:row + CH, 4 * w * S:(4 * w + 4) * S]
                                    src = qk["k_" + part][w * HALF:(w + 1) * HALF, e * S:(e + 1) * S]
                                    eng.dma_start(dst.bitcast(F32).rearrange("c (t n) -> c t n", t=4), src.bitcast(F32))\
                                       .then_inc(s_kst[w][b.par], 16)

                        def place_max(b, w):
                            e_mlo.wait(eng, b, w + 1)
                            for c, row in enumerate((ROW_HI, ROW_LO)):
                                dst = qs[b.par][row::HALF, 4 * w * S:(4 * w + 4) * S]
                                eng.dma_start(dst.bitcast(F32).rearrange("p (t n) -> p t n", t=4),
                                              mhl[w][:, c * S:(c + 1) * S].bitcast(F32)).then_inc(s_mdma[w][b.par], 16)

                        def load_gates(b):
                            e_res.wait(eng, b.back(UNROLL))
                            eng.dma_start(gbc[b.par][:, :], gd[b.pair, b.par].partition_broadcast(P))\
                               .then_inc(s_gin[b.par], 16)

                        T_SP = {"k0": 10, "k1": 21.5, "M0": 26, "M1": 38.5, "gates": 41}
                        tasks = {"k0": lambda b: place_k(b, 0), "k1": lambda b: place_k(b, 1),
                                 "M0": lambda b: place_max(b, 0), "M1": lambda b: place_max(b, 1), "gates": load_gates}
                        tasks["D w1"] = lambda b: preload(eng, [staged["D"]["w1"]])
                        run_tasks(eng, schedule(EARLY, T_SP, {"D w1": 44}), tasks, once=("D w1",))

        with nc.sbuf_tensor("stage1", [P, STAGE], F32) as second_half:
            stage.append(second_half)
            phase_l0_attention()
            phase_mlp(0)
            stage.pop()
        phase_l1_attention()
        with nc.sbuf_tensor("stage1d", [P, STAGE], F32) as second_half:
            stage.append(second_half)
            phase_mlp(1)


def kernel(**inputs):
    import numpy as np
    import concourse.bacc as bacc
    from concourse.bass_utils import run_bass_kernel_spmd

    nc = bacc.Bacc("TRN2", target_bir_lowering=False, num_devices=1)
    arrays, aps = {}, {}
    for name, value in inputs.items():
        v = np.ascontiguousarray(value)
        arrays[f"in_{name}"] = v
        aps[name] = nc.dram_tensor(f"in_{name}", v.shape, mybir.dt.from_np(v.dtype), kind="ExternalInput").ap()
    out = nc.dram_tensor("out", aps["x"].shape, F32, kind="ExternalOutput").ap()
    nb, _, d = aps["x"].shape
    mod_dram = nc.dram_tensor("mod_rows", [3, nb, 2 * d], F32, kind="Internal").ap()
    build(nc, aps, out, mod_dram)
    r = run_bass_kernel_spmd(nc, [arrays], core_ids=[0])
    return r.results[0]["out"]
```
